# Optimizing a Trainium2 kernel written in Bass

```python
import numpy as np
import jax
import jax.numpy as jnp

def _softmax(x, axis=-1):
    return jax.nn.softmax(x, axis=axis)
def _gelu(x):
    return jax.nn.gelu(x, approximate=True)
def _silu(x):
    return jax.nn.silu(x)
def _sigmoid(x):
    return jax.nn.sigmoid(x)
def _layernorm(x, axis=-1, eps=1e-5):
    m = jnp.mean(x, axis=axis, keepdims=True)
    v = jnp.var(x, axis=axis, keepdims=True)
    return (x - m) / jnp.sqrt(v + eps)
def _scatter_add(tgt, idx, src, axis=0):
    return tgt.at[idx].add(src)
def _segment_sum(src, seg, n):
    return jax.ops.segment_sum(src, seg, n)

kernel_name = 'mk_conv_attn_hybrid_d2_conv_nhwc128_0743a1'

def setup_inputs(seed: int = 0):
    np.random.seed(seed)
    _w = jnp.asarray
    def _rec_inputs():
        import jax
        import jax.numpy as jnp
        _gk = jax.random.key(seed)
        x = -0.0005207 + 1.001 * jax.random.normal(jax.random.fold_in(_gk, 1), (4, 64, 64, 128), jnp.float32)
        return x
    x = _rec_inputs()
    def _L0_conv_setup():
        import jax, jax.numpy as jnp
        import numpy as np
        B, H, W, C, R = (4, 64, 64, 128, 8)
        D = C // R
        key = jax.random.key(seed)
        k1, k2, k3, k4, k5 = jax.random.split(key, 5)
        x = jax.random.normal(k1, (B, H, W, C), dtype=jnp.float32)
        Wq = jax.random.normal(k2, (C, D), dtype=jnp.float32) * 0.05
        Wk = jax.random.normal(k3, (C, D), dtype=jnp.float32) * 0.05
        Wv = jax.random.normal(k4, (C, C), dtype=jnp.float32) * 0.05
        gamma = jax.random.normal(k5, (), dtype=jnp.float32)
        return {'x': x, 'Wq': Wq, 'Wk': Wk, 'Wv': Wv, 'gamma': gamma}
    _L0_conv_all = _L0_conv_setup()
    _L0_conv_in = {k: v for k, v in _L0_conv_all.items() if k in ('Wq', 'Wk', 'Wv', 'gamma', )}
    del _L0_conv_all

    def _L1_attn_setup():
        import jax, jax.numpy as jnp
        import numpy as np
        HEADS = 8
        DIM = 128
        key = jax.random.key(seed)
        k1, k2, k3 = jax.random.split(key, 3)
        b, t, d, h = (4, 4096, DIM, HEADS)
        x = jax.random.normal(k1, (b, t, d), dtype=jnp.float32)
        W_kv = jax.random.normal(k2, (h * d * 2, d), dtype=jnp.float32) * (1.0 / np.sqrt(d))
        q_proj = jax.random.normal(k3, (h, d), dtype=jnp.float32) * (1.0 / np.sqrt(d))
        return {'x': x, 'W_kv': W_kv, 'q_proj': q_proj}
    _L1_attn_all = _L1_attn_setup()
    _L1_attn_in = {k: v for k, v in _L1_attn_all.items() if k in ('W_kv', 'q_proj', )}
    del _L1_attn_all

    def _L1_ffn_setup():
        import jax, jax.numpy as jnp
        import numpy as np
        B, S, D, E, H, O, K = (512, 2048, 128, 64, 512, 128, 8)
        key = jax.random.key(seed)
        k0, k1, k2, k3 = jax.random.split(key, 4)
        x = jax.random.normal(k0, (B, S, D), dtype=jnp.float32)
        gate_w = jax.random.normal(k1, (E, D), dtype=jnp.float32) * (1.0 / np.sqrt(D))
        gate_b = jnp.zeros((E,), dtype=jnp.float32)
        weight1 = jax.random.uniform(k2, (E, D + 1, H), dtype=jnp.float32, minval=-1.0, maxval=1.0) * (1.0 / np.sqrt(D + 1))
        weight2 = jax.random.uniform(k3, (E, H + 1, O), dtype=jnp.float32, minval=-1.0, maxval=1.0) * (1.0 / np.sqrt(H + 1))
        return {'x': x, 'gate_w': gate_w, 'gate_b': gate_b, 'weight1': weight1, 'weight2': weight2}
    _L1_ffn_all = _L1_ffn_setup()
    _L1_ffn_in = {k: v for k, v in _L1_ffn_all.items() if k in ('gate_w', 'gate_b', 'weight1', 'weight2', )}
    del _L1_ffn_all

    return {
        "x": x,
        "L0_conv_Wq": _L0_conv_in["Wq"],
        "L0_conv_Wk": _L0_conv_in["Wk"],
        "L0_conv_Wv": _L0_conv_in["Wv"],
        "L0_conv_gamma": _L0_conv_in["gamma"],
        "L1_attn_W_kv": _L1_attn_in["W_kv"],
        "L1_attn_q_proj": _L1_attn_in["q_proj"],
        "L1_ffn_gate_w": _L1_ffn_in["gate_w"],
        "L1_ffn_gate_b": _L1_ffn_in["gate_b"],
        "L1_ffn_weight1": _L1_ffn_in["weight1"],
        "L1_ffn_weight2": _L1_ffn_in["weight2"],
    }

def reference(x, L0_conv_Wq, L0_conv_Wk, L0_conv_Wv, L0_conv_gamma, L1_attn_W_kv, L1_attn_q_proj, L1_ffn_gate_w, L1_ffn_gate_b, L1_ffn_weight1, L1_ffn_weight2):
    import jax
    import jax.numpy as jnp
    def _L0_conv_ref(x, Wq, Wk, Wv, gamma):
        import jax, jax.numpy as jnp
        import numpy as np
        B, H, W, C, R = (4, 64, 64, 128, 8)
        D = C // R
        b, h, w, c = x.shape
        n = h * w
        xf = x.reshape(b, n, c)
        f = jnp.einsum('bnc,cd->bnd', xf, Wq)
        g = jnp.einsum('bnc,cd->bnd', xf, Wk)
        hv = jnp.einsum('bnc,ce->bne', xf, Wv)
        scores = jnp.einsum('bnd,bmd->bnm', f, g)
        beta = jax.nn.softmax(scores, axis=1)
        att = jnp.einsum('bnc,bnm->bcm', hv, beta)
        att = att.reshape(b, h, w, c)
        return gamma * att + x

    def _L1_attn_ref(x, W_kv, q_proj):
        import jax, jax.numpy as jnp
        import numpy as np
        HEADS = 8
        DIM = 128
        b, t, d = x.shape
        h = q_proj.shape[0]
        kv = jnp.einsum('btd,ed->bte', x, W_kv).reshape(b, t, h, d, 2)
        kv = jax.nn.silu(kv)
        k, v = (kv[..., 0], kv[..., 1])
        s = jnp.einsum('hd,bthd->bth', q_proj, k)
        m_A = jax.lax.cummax(s, axis=1)
        exp_scores = jnp.exp(s - m_A)
        u_A = jnp.cumsum(exp_scores, axis=1)
        w_A = jnp.cumsum(exp_scores[..., None] * v, axis=1)
        output = w_A / u_A[..., None]
        return output.mean(axis=2)

    def _L1_ffn_ref(x, gate_w, gate_b, weight1, weight2):
        import jax, jax.numpy as jnp
        import numpy as np
        B, S, D, E, H, O, K = (512, 2048, 128, 64, 512, 128, 8)
        Bn, Sn, Dn = x.shape
        logits = jnp.einsum('bsd,ed->bse', x, gate_w) + gate_b
        probs = jax.nn.softmax(logits, axis=1)
        vals, idx = jax.lax.top_k(probs.transpose(0, 2, 1), K)
        topv = vals.transpose(0, 2, 1)
        topi = idx.transpose(0, 2, 1)
        flat_idx = topi.reshape(Bn, K * E)
        gathered = jnp.take_along_axis(x, flat_idx[:, :, None], axis=1)
        gathered = gathered.reshape(Bn, K, E, Dn)
        pooled = jnp.einsum('bked,bke->bed', gathered, topv)
        ones = jnp.ones((E, Bn, 1), dtype=x.dtype)
        h = jnp.concatenate([pooled.transpose(1, 0, 2), ones], axis=-1)
        h = jax.nn.gelu(jnp.einsum('ebd,edh->ebh', h, weight1), approximate=False)
        h = jnp.concatenate([h, ones], axis=-1)
        out = jnp.einsum('ebh,eho->ebo', h, weight2)
        out = out.transpose(1, 0, 2)
        weighted = jnp.einsum('beo,bke->bkeo', out, topv).reshape(Bn, K * E, O)
        outputs = jnp.zeros((Bn, Sn, O), dtype=x.dtype)
        outputs = outputs.at[jnp.arange(Bn)[:, None], flat_idx].add(weighted)
        return outputs

    def _gn(v, G=32, eps=1e-5):
        B_, H_, W_, C_ = v.shape
        g = v.reshape(B_, H_, W_, G, C_ // G)
        m = jnp.mean(g, axis=(1, 2, 4), keepdims=True)
        s = jnp.var(g, axis=(1, 2, 4), keepdims=True)
        return ((g - m) / jnp.sqrt(s + eps)).reshape(v.shape)

    def _ln_c(v, eps=1e-6):
        m = jnp.mean(v, axis=-1, keepdims=True)
        s = jnp.var(v, axis=-1, keepdims=True)
        return (v - m) / jnp.sqrt(s + eps)

    def _ln_t(v, eps=1e-5):
        m = jnp.mean(v, axis=-1, keepdims=True)
        s = jnp.var(v, axis=-1, keepdims=True)
        return (v - m) / jnp.sqrt(s + eps)

    def _to_tokens(v):
        B_, H_, W_, C_ = v.shape
        return v.reshape(B_, H_ * W_, C_)
    def _from_tokens(t, like):
        return t.reshape(like.shape)

    x = _L0_conv_ref(x, L0_conv_Wq, L0_conv_Wk, L0_conv_Wv, L0_conv_gamma)
    t = _to_tokens(x)
    t = t + _L1_attn_ref(_ln_t(t), L1_attn_W_kv, L1_attn_q_proj)
    t = t + _L1_ffn_ref(_ln_t(t), L1_ffn_gate_w, L1_ffn_gate_b, L1_ffn_weight1, L1_ffn_weight2)
    x = _from_tokens(t, x)
    return x


_drawn_inputs = setup_inputs


def setup_inputs(seed=0):
    import zlib

    import numpy as np

    out = dict(_drawn_inputs(seed))
    spreads = {'L1_ffn_gate_b': (0.0, 0.8)}
    factors = {'L1_attn_W_kv': 3.507,
     'L1_attn_q_proj': 5.834,
     'L1_ffn_gate_w': 8.0,
     'L1_ffn_weight1': 6.098,
     'L1_ffn_weight2': 5.663}
    for name, (base, spread) in spreads.items():
        noise = np.random.default_rng([zlib.crc32(name.encode()), seed]).standard_normal(out[name].shape)
        drawn = base * np.exp(spread * noise) if base else spread * noise
        out[name] = jnp.asarray(drawn.astype(out[name].dtype))
    for name, factor in factors.items():
        out[name] = (out[name] * factor).astype(out[name].dtype)
    return out
```

```python
import concourse.bass as bass
from concourse import mybir
from contextlib import ExitStack

ALU = mybir.AluOpType
ACT = mybir.ActivationFunctionType
AX = mybir.AxisListType
F32 = mybir.dt.float32
F32R = mybir.dt.float32r

P = 128
BANK = 512
PARTS = 4
DMA = 16


def plain(ap):
    return ap.bitcast(F32)


class Program:

    def __init__(self, nc, whole, ins, out):
        self.nc, self.whole, self.ins, self.out = nc, whole, ins, out
        self.B, self.H, self.W, self.C = ins["x"].shape
        self.N = self.H * self.W
        self.D = ins["L0_conv_Wq"].shape[1]
        self.NT = self.N // P
        self.KR = PARTS * self.D + 2
        scratch = lambda name, shape, dt: nc.dram_tensor(name, shape, dt).ap()
        self.f_d = scratch("f_scratch", (self.KR, self.B * self.N), F32)
        self.g_d = scratch("g_scratch", (self.KR, self.B * self.N), F32)
        self.hv_d = scratch("hv_scratch", (P, self.B * self.N), F32)
        self.y_d = scratch("y_scratch", (self.B * self.N * self.C + self.N,), F32)
        self.y_tok = self.y_d[0:self.B * self.N * self.C].rearrange("(t c) -> t c", c=self.C)
        self.t2_d = scratch("t2_scratch", (self.B * self.N, self.C), F32)
        self.HEADS = ins["L1_attn_q_proj"].shape[0]
        self.E = ins["L1_ffn_gate_w"].shape[0]
        self.chosen_d = scratch("chosen_scratch", (self.E, self.B * self.N), F32)
        self.expert_d = scratch("expert_scratch", (self.E, self.B, self.C), F32)

    def sem(self, name):
        return self.whole.enter_context(self.nc.semaphore(name))

    def const(self, name, shape, dt=F32):
        return self.whole.enter_context(self.nc.sbuf_tensor(name, shape, dt))


def wait_first(engine, passed, *waits):
    waits = [(sem, engine.to_reg(value)) for sem, value in waits]
    engine.wait_ge(passed, 1)
    for sem, value in waits:
        engine.wait_ge(sem, value)


def prepare(p):
    nc, C, D = p.nc, p.C, p.D
    p.ident = p.const("ident", [P, P])
    p.ones = p.const("ones", [P, P])
    p.wf = p.const("wf", [C, PARTS * D])
    p.wg = p.const("wg", [C, PARTS * D])
    p.wv = p.const("wv", [C, C])
    p.low_f = p.const("low_f", [PARTS * D, 1])
    p.low_g = p.const("low_g", [PARTS * D, 1])
    p.low_2 = p.const("low_2", [2, 1])
    p.gamma = p.const("gamma", [P, 1])
    with ExitStack() as ctx:
        sb = lambda n, s, dt=F32: ctx.enter_context(nc.sbuf_tensor(n, s, dt))
        wq = sb("wq", [C, D])
        wk = sb("wk", [C, D])
        steps = sb("steps", [PARTS * D, 3])
        loaded = p.sem("prep_loaded")
        filled = p.sem("prep_filled")
        chosen = p.sem("prep_chosen")
        stepped = p.sem("prep_stepped")
        block = ctx.enter_context(nc.Block())

        @block.sync
        def _(sp):
            sp.dma_start(wq[:], p.ins["L0_conv_Wq"]).then_inc(loaded, DMA)
            sp.dma_start(wk[:], p.ins["L0_conv_Wk"]).then_inc(loaded, DMA)
            sp.dma_start(p.wv[:], p.ins["L0_conv_Wv"]).then_inc(loaded, DMA)
            sp.dma_start(p.gamma[:], p.ins["L0_conv_gamma"].partition_broadcast(P)).then_inc(loaded, DMA)
            sp.wait_ge(loaded, 4 * DMA)

        @block.gpsimd
        def _(pool):
            nc.gpsimd.memset(p.ident[:], 0.0).then_inc(filled, 1)
            nc.gpsimd.memset(p.ones[:], 1.0).then_inc(filled, 1)
            nc.gpsimd.memset(steps[:], 1.0).then_inc(filled, 1)
            nc.gpsimd.memset(p.low_2[:], 1.0).then_inc(filled, 1)
            pool.wait_ge(filled, 4)
            nc.gpsimd.affine_select(out=p.ident[:], in_=p.ident[:], compare_op=ALU.not_equal, fill=1.0, base=0,
                                    pattern=[[-1, P]], channel_multiplier=1).then_inc(chosen, 1)
            nc.gpsimd.affine_select(out=steps[:], in_=steps[:], compare_op=ALU.is_ge, fill=0.0, base=-D,
                                    pattern=[[-D, 3]], channel_multiplier=1).then_inc(chosen, 1)
            nc.gpsimd.affine_select(out=p.low_2[:], in_=p.low_2[:], compare_op=ALU.is_ge, fill=0.0, base=-1,
                                    pattern=[[0, 1]], channel_multiplier=1).then_inc(chosen, 1)

        @block.vector
        def _(dve):
            dve.wait_ge(chosen, 3)
            nc.vector.tensor_copy(p.low_f[:], steps[:, 1:2])
            nc.vector.tensor_tensor(p.low_g[:], steps[:, 0:1], steps[:, 1:2], ALU.subtract).then_inc(stepped, 1)
            dve.wait_ge(stepped, 1)
            nc.vector.tensor_tensor(p.low_g[:], p.low_g[:], steps[:, 2:3], ALU.add)

        @block.scalar
        def _(act):
            act.wait_ge(loaded, 4 * DMA)
            for part in range(PARTS):
                cols = slice(part * D, (part + 1) * D)
                nc.scalar.mul(p.wf[:, cols], wq[:], -1.0 if part < 2 else 1.0)
                nc.scalar.mul(p.wg[:, cols], wk[:], -1.0 if part % 2 == 0 else 1.0)


def project(p):
    nc, B, C, N, R, KR = p.nc, p.B, p.C, p.N, PARTS * p.D, p.KR
    TILES = BANK // P
    CHUNKS = p.NT // TILES
    x_v = p.ins["x"].rearrange("b h w c -> b (h w c)").rearrange("b (p n) -> b p n", p=P)
    with ExitStack() as ctx:
        sb = lambda n, s, dt=F32: ctx.enter_context(nc.sbuf_tensor(n, s, dt))
        ps = lambda n, s: ctx.enter_context(nc.psum_tensor(n, s, F32))
        xin = [sb(f"xin{i}", [P, BANK]) for i in range(2)]
        xt = [sb(f"xt{i}", [P, BANK]) for i in range(2)]
        f_high = [sb(f"f_high{i}", [R, BANK], F32R) for i in range(2)]
        g_high = [sb(f"g_high{i}", [R, BANK], F32R) for i in range(2)]
        f_rows = [sb(f"f_rows{i}", [KR, BANK], F32R) for i in range(2)]
        hv = [sb(f"hv{i}", [P, BANK]) for i in range(2)]
        g_rows = sb("g_rows", [KR, B * N], F32R)
        xt_ps = [ps(f"xt_ps{i}", [P, BANK]) for i in range(2)]
        f_ps = [ps(f"f_ps{i}", [P, BANK]) for i in range(2)]
        g_ps = [ps(f"g_ps{i}", [P, BANK]) for i in range(2)]
        hv_ps = [ps(f"hv_ps{i}", [P, BANK]) for i in range(2)]
        x_loaded = [p.sem(f"x_loaded{i}") for i in range(2)]
        x_turned = p.sem("x_turned")
        xt_ready = p.sem("xt_ready")
        f_made, g_made, hv_made = p.sem("f_made"), p.sem("g_made"), p.sem("hv_made")
        f_rounded, g_rounded = p.sem("f_rounded"), p.sem("g_rounded")
        f_split, g_split = p.sem("f_split"), p.sem("g_split")
        hv_ready = p.sem("hv_ready")
        f_stored = [p.sem(f"f_stored{i}") for i in range(2)]
        hv_stored = [p.sem(f"hv_stored{i}") for i in range(2)]
        g_stored = p.sem("g_stored")
        filled = p.sem("rows_filled")
        PAIRS = B * CHUNKS // 2
        block = ctx.enter_context(nc.Block())

        @block.sync
        def _(sp):
            with sp.Fori(0, B) as b:
                with sp.Fori(0, CHUNKS // 2) as c2:
                    for i in range(2):
                        n = b * (CHUNKS // 2) + c2
                        sp.wait_ge(x_turned, 2 * n + i)
                        sp.dma_start(xin[i][:], x_v[b, :, bass.ds((2 * c2 + i) * BANK, BANK)]).then_inc(x_loaded[i], DMA)

        @block.tensor
        def _(pe):
            with pe.Fori(0, PAIRS) as n:
                for i in range(2):
                    pe.wait_ge(x_loaded[i], DMA * (n + 1))
                    pe.wait_ge(xt_ready, 2 * n + i)
                    for t in range(TILES):
                        last = nc.tensor.transpose(xt_ps[i][:, t * P:(t + 1) * P], xin[i][:, t * P:(t + 1) * P], p.ident[:])
                    last.then_inc(x_turned, 1)
                    pe.wait_ge(xt_ready, 2 * n + i + 1)
                    pe.wait_ge(f_split, 2 * n + i)
                    nc.tensor.matmul(f_ps[i][0:R, :], p.wf[:], xt[i][:], start=True, stop=True).then_inc(f_made, 1)
                    pe.wait_ge(g_split, 2 * n + i)
                    nc.tensor.matmul(g_ps[i][0:R, :], p.wg[:], xt[i][:], start=True, stop=True).then_inc(g_made, 1)
                    pe.wait_ge(hv_ready, 2 * n + i)
                    for t in range(TILES):
                        last = nc.tensor.matmul(hv_ps[i][:, t * P:(t + 1) * P], xt[i][:, t * P:(t + 1) * P], p.wv[:],
                                                start=True, stop=True)
                    last.then_inc(hv_made, 1)

        @block.vector
        def _(dve):
            for i in range(2):
                nc.vector.memset(plain(f_rows[i][R:KR, :]), 1.0).then_inc(filled, 1)
            nc.vector.memset(plain(g_rows[R:KR, :]), 0.0).then_inc(filled, 1)
            with dve.Fori(0, PAIRS) as n:
                for i in range(2):
                    dve.wait_ge(f_made, 2 * n + i + 1)
                    nc.vector.tensor_copy(f_high[i][:], f_ps[i][0:R, :]).then_inc(f_rounded, 1)
                    dve.wait_ge(g_made, 2 * n + i + 1)
                    nc.vector.tensor_copy(g_high[i][:], g_ps[i][0:R, :]).then_inc(g_rounded, 1)
                    dve.wait_ge(f_rounded, 2 * n + i + 1)
                    dve.wait_ge(f_stored[i], DMA * n)
                    nc.vector.scalar_tensor_tensor(f_rows[i][0:R, :], f_ps[i][0:R, :], p.low_f[:], plain(f_high[i][:]),
                                                   ALU.mult, ALU.subtract).then_inc(f_split, 1)
                    dve.wait_ge(g_rounded, 2 * n + i + 1)
                    b, c = n // (CHUNKS // 2), n % (CHUNKS // 2)
                    rows = g_rows[0:R, bass.ds(b * N, N)].rearrange("r (q t) -> r t q", t=p.NT)
                    rows = rows[:, bass.ds((2 * c + i) * TILES, TILES), :]
                    nc.vector.scalar_tensor_tensor(
                        rows, g_ps[i][0:R, :].rearrange("r (t q) -> r t q", q=P), p.low_g[:],
                        plain(g_high[i][:]).rearrange("r (t q) -> r t q", q=P), ALU.mult, ALU.subtract).then_inc(g_split, 1)

        @block.scalar
        def _(act):
            act.wait_ge(filled, 3)
            with act.Fori(0, B) as b:
                with act.Fori(0, CHUNKS // 2) as c2:
                    for i in range(2):
                        n = b * (CHUNKS // 2) + c2
                        columns = bass.ds(b * N + (2 * c2 + i) * BANK, BANK)
                        act.wait_ge(x_turned, 2 * n + i + 1)
                        act.wait_ge(hv_made, 2 * n + i)
                        nc.scalar.copy(xt[i][:], xt_ps[i][:]).then_inc(xt_ready, 1)
                        act.wait_ge(hv_made, 2 * n + i + 1)
                        act.wait_ge(hv_stored[i], DMA * n)
                        nc.scalar.copy(hv[i][:], hv_ps[i][:]).then_inc(hv_ready, 1)
                        act.wait_ge(f_split, 2 * n + i + 1)
                        act.dma_start(p.f_d[:, columns], plain(f_rows[i][:])).then_inc(f_stored[i], DMA)
                        act.wait_ge(hv_ready, 2 * n + i + 1)
                        act.dma_start(p.hv_d[:, columns], hv[i][:]).then_inc(hv_stored[i], DMA)
                act.wait_ge(g_split, (b + 1) * CHUNKS)
                act.dma_start(p.g_d[:, bass.ds(b * N, N)], plain(g_rows[:, bass.ds(b * N, N)])).then_inc(g_stored, DMA)
            for i in range(2):
                act.wait_ge(f_stored[i], DMA * PAIRS)
                act.wait_ge(hv_stored[i], DMA * PAIRS)
            act.wait_ge(g_stored, B * DMA)


def pairs(p):
    nc, B, C, N, R, KR = p.nc, p.B, p.C, p.N, PARTS * p.D, p.KR
    M = 2 * BANK
    BLOCKS = B * N // M
    PER_IMAGE = N // M
    GROUP = 4
    GROUPS = p.NT // GROUP
    HALVES = M // BANK
    assert GROUPS * P == M and BLOCKS % 2 == 0 and GROUPS % 2 == 0
    USES = GROUPS * (2 * GROUP + 1) + HALVES
    FIRST_USES = GROUPS * (2 * GROUP + 1)
    x_v = p.ins["x"].rearrange("b h w c -> b (h w c)").rearrange("b (p n) -> b p n", p=P)
    with ExitStack() as ctx:
        sb = lambda n, s, dt=F32: ctx.enter_context(nc.sbuf_tensor(n, s, dt))
        ps = lambda n, s: ctx.enter_context(nc.psum_tensor(n, s, F32))
        f_all = [sb(f"f_all{i}", [KR, N], F32R) for i in range(2)]
        g_cols = [sb(f"g_cols{i}", [KR, M], F32R) for i in range(2)]
        f_tiles = [sb(f"f_tiles{i}", [KR, GROUP * P], F32R) for i in range(2)]
        hv_tiles = [sb(f"hv_tiles{i}", [P, GROUP * P]) for i in range(2)]
        g_tile = [sb(f"g_tile{i}", [KR, P], F32R) for i in range(2)]
        probs = [sb(f"probs{i}", [P, M]) for i in range(GROUP)]
        sums = [sb(f"sums{i}", [P, M]) for i in range(2)]
        x_res = [sb(f"x_res{i}", [P, M]) for i in range(2)]
        att_sb = [sb(f"att_sb{i}", [P, M]) for i in range(2)]
        y_out = [sb(f"y_out{i}", [P, M]) for i in range(2)]
        inv = sb("inv", [P, M])
        part_max = sb("part_max", [P, 2 * GROUP])
        pm_max = sb("pm_max", [P, 2])
        row = sb("row", [2, P])
        row_high = sb("row_high", [2, P], F32R)
        scores = [ps(f"scores{i}", [P, M]) for i in range(2)]
        att = ps("att", [P, M])
        side = [ps(f"side{i}", [P, BANK]) for i in range(2)]

        tiles_loaded = [p.sem(f"tiles_loaded{i}") for i in range(2)]
        g_tile_loaded = [p.sem(f"g_tile_loaded{i}") for i in range(2)]
        f_loaded = [p.sem(f"f_loaded{i}") for i in range(2)]
        g_loaded = [p.sem(f"g_loaded{i}") for i in range(2)]
        x_res_loaded = [p.sem(f"x_res_loaded{i}") for i in range(2)]
        scored, exped = p.sem("scored"), p.sem("exped")
        weighed, summed = p.sem("weighed"), p.sem("summed")
        side_full, side_free = p.sem("side_full"), p.sem("side_free")
        max_ready, shift_ready = p.sem("max_ready"), p.sem("shift_ready")
        row_step = p.sem("row_step")
        att_copied = p.sem("att_copied")
        norm_step = p.sem("norm_step")
        y_ready = p.sem("y_ready")
        y_stored = [p.sem(f"y_stored{i}") for i in range(2)]
        block = ctx.enter_context(nc.Block())

        def image(k):
            return k // PER_IMAGE

        def first_column(k):
            return (k % PER_IMAGE) * M

        def each_block(engine, run):
            with engine.Fori(0, BLOCKS // 2 - 1) as pair:
                run(2 * pair, 0, pair)
                run(2 * pair + 1, 1, pair)
            run(BLOCKS - 2, 0, BLOCKS // 2 - 1)
            run(BLOCKS - 1, 1, BLOCKS // 2 - 1)

        def is_from(k, block):
            return isinstance(k, int) and k >= block

        def each_group(engine, run):
            run(0, 0, 0)
            with engine.Fori(0, GROUPS // 2 - 1) as g2:
                run(2 * g2 + 1, 1, g2)
                run(2 * g2 + 2, 0, g2 + 1)
            run(GROUPS - 1, 1, GROUPS // 2 - 1)

        def is_group(gi, which):
            return isinstance(gi, int) and gi == which

        def first_use(k):
            return k * USES + FIRST_USES

        TILE_USES = 2 * GROUP + 1
        FILLS = GROUPS // 2

        @block.sync
        def _(sp):
            def load_f(first, i):
                sp.dma_start(plain(f_all[i][:]), p.f_d[:, bass.ds(first, N)]).then_inc(f_loaded[i], DMA)

            def load_g(first, i):
                sp.dma_start(plain(g_cols[i][0:R, :]), p.g_d[0:R, bass.ds(first, M)]).then_inc(g_loaded[i], DMA)

            def load_g_tile(first, slot):
                sp.dma_start(plain(g_tile[slot][:]), p.g_d[:, bass.ds(first, P)]).then_inc(g_tile_loaded[slot], DMA)

            load_f(0, 0)
            load_g(0, 0)
            load_f(image(1) * N, 1)
            with sp.Fori(0, GROUPS // 2) as g2:
                for slot in range(2):
                    first = sp.snap((2 * g2 + slot) * P)
                    sp.wait_ge(max_ready, 2 * g2 + slot)
                    load_g_tile(first, slot)

            def run(k, i, pair):
                def group(gi, slot, filling):
                    g = k * GROUPS + gi
                    tiles_at = sp.snap(image(k) * N + gi * (GROUP * P))
                    tile_at = sp.snap((k + 1) * M + gi * P)
                    g_at = sp.snap((k + 1) * M)
                    f_at = sp.snap(image(k + 2) * N)
                    sp.wait_ge(weighed, g * GROUP + GROUP)
                    sp.dma_start(plain(f_tiles[slot][:]), p.f_d[:, bass.ds(tiles_at, GROUP * P)]).then_inc(tiles_loaded[slot], DMA)
                    sp.dma_start(hv_tiles[slot][:], p.hv_d[:, bass.ds(tiles_at, GROUP * P)]).then_inc(tiles_loaded[slot], DMA)
                    if not is_from(k, BLOCKS - 1):
                        sp.wait_ge(max_ready, g + GROUPS)
                        load_g_tile(tile_at, slot)
                    if is_group(gi, 0) and not is_from(k, BLOCKS - 1):
                        sp.wait_ge(weighed, k * p.NT + 2 * GROUP)
                        load_g(g_at, 1 - i)
                        if not is_from(k, BLOCKS - 2):
                            sp.wait_ge(max_ready, (k + 1) * GROUPS + 1)
                            load_f(f_at, i)
                    if is_group(gi, GROUPS - 1) and not (isinstance(k, int) and k == 0):
                        store_y(k - 1, 1 - i)
                each_group(sp, group)

            def store_y(k, i):
                at = sp.snap(image(k) * (P * N) + first_column(k))
                target = p.y_d[bass.ds(at, P * N)].rearrange("(p n) -> p n", p=P)[:, 0:M]
                sp.wait_ge(y_ready, k + 3)
                sp.dma_start(target, y_out[i][:]).then_inc(y_stored[i], DMA)

            run(0, 0, 0)
            run(1, 1, 0)
            with sp.Fori(1, BLOCKS // 2 - 1) as pair:
                run(2 * pair, 0, pair)
                run(2 * pair + 1, 1, pair)
            run(BLOCKS - 2, 0, BLOCKS // 2 - 1)
            run(BLOCKS - 1, 1, BLOCKS // 2 - 1)
            store_y(BLOCKS - 1, 1)
            for i in range(2):
                sp.wait_ge(y_stored[i], DMA * (BLOCKS // 2))

        @block.tensor
        def _(pe):
            pe.sem_inc(weighed, 2 * GROUP)

            def chunk(use, slot, side_i, c):
                pe.wait_ge(side_free, use)
                nc.tensor.matmul(side[c % 2][:], g_tile[slot][:], f_all[side_i][:, c * BANK:(c + 1) * BANK],
                                 start=True, stop=True).then_inc(side_full, 1)

            def shift_rows(tile):
                pe.wait_ge(max_ready, tile + 2)
                nc.tensor.matmul(side[1][0:2, 0:P], pm_max[:], p.ident[:], start=True, stop=True).then_inc(side_full, 1)

            pe.wait_ge(f_loaded[0], DMA)
            with pe.Fori(0, GROUPS // 2) as g2:
                for slot in range(2):
                    tile = 2 * g2 + slot
                    pe.wait_ge(g_tile_loaded[slot], DMA * (g2 + 1))
                    for c in range(2 * GROUP):
                        chunk(tile * TILE_USES + c, slot, 0, c)
                    shift_rows(tile)

            def run(k, i, pair):
                last = is_from(k, BLOCKS - 1)
                use = first_use(k)
                pe.wait_ge(shift_ready, (k + 1) * GROUPS)
                pe.wait_ge(g_loaded[i], DMA * (pair + 1))

                def weigh(t, s, slot, first=False, final=False):
                    pe.wait_ge(exped, t + 1)
                    if first:
                        pe.wait_ge(att_copied, k)
                    for h in range(HALVES):
                        cols = slice(h * BANK, (h + 1) * BANK)
                        done = nc.tensor.matmul(att[:, cols], hv_tiles[slot][:, s * P:(s + 1) * P], probs[s][:, cols],
                                                start=first, stop=final)
                    done.then_inc(weighed, 1)

                def group(gi, slot, filling):
                    g = k * GROUPS + gi
                    pe.wait_ge(tiles_loaded[slot], 2 * DMA * (k * FILLS + filling + 1))
                    if not last:
                        pe.wait_ge(g_tile_loaded[slot], DMA * ((k + 1) * FILLS + filling + 1))
                        if is_group(gi, 0):
                            pe.wait_ge(f_loaded[1 - i], DMA * (pair + 1 + i))
                    for s in range(GROUP):
                        t = g * GROUP + s
                        for h in range(HALVES):
                            cols = slice(h * BANK, (h + 1) * BANK)
                            done = nc.tensor.matmul(scores[s % 2][:, cols], f_tiles[slot][:, s * P:(s + 1) * P],
                                                    g_cols[i][:, cols], start=True, stop=True)
                        done.then_inc(scored, 1)
                        if s > 0:
                            weigh(t - 1, s - 1, slot, first=is_group(gi, 0) and s == 1)
                        elif not is_group(gi, 0):
                            weigh(t - 1, GROUP - 1, 1 - slot)
                            if not last:
                                shift_rows(g + GROUPS - 1)
                        if not last:
                            for c in (2 * s, 2 * s + 1):
                                chunk(use + gi * TILE_USES + c, slot, 1 - i, c)

                each_group(pe, group)
                weigh((k + 1) * p.NT - 1, GROUP - 1, 1, final=True)
                if not last:
                    shift_rows((k + 2) * GROUPS - 1)
                    use = use + GROUPS * TILE_USES
                pe.wait_ge(summed, (k + 1) * p.NT + GROUP)
                for h in range(HALVES):
                    pe.wait_ge(side_free, use + h)
                    nc.tensor.matmul(side[h][:], p.ones[:], sums[i][:, h * BANK:(h + 1) * BANK],
                                     start=True, stop=True).then_inc(side_full, 1)
            each_block(pe, run)

        @block.scalar
        def _(act):
            def run(k, i, pair):
                act.wait_ge(y_ready, k + 1)
                act.dma_start(x_res[i][:], x_v[image(k), :, bass.ds(first_column(k), M)]).then_inc(x_res_loaded[i], DMA)

                def group(gi, slot, filling):
                    for s in range(GROUP):
                        t = (k * GROUPS + gi) * GROUP + s
                        act.wait_ge(scored, t + 1)
                        act.wait_ge(weighed, t + 1 + GROUP)
                        act.wait_ge(summed, t + 1)
                        nc.scalar.activation(probs[s][:], scores[s % 2][:], ACT.Exp).then_inc(exped, 1)
                each_group(act, group)
                act.wait_ge(weighed, (k + 1) * p.NT + 2 * GROUP)
                nc.scalar.copy(att_sb[i][:], att[:]).then_inc(att_copied, 1)
            each_block(act, run)

        @block.gpsimd
        def _(pool):
            pool.sem_inc(summed, GROUP)

            def run(k, i, pair):
                def group(gi, slot, filling):
                    for s in range(GROUP):
                        t = (k * GROUPS + gi) * GROUP + s
                        pool.wait_ge(exped, t + 1)
                        if is_group(gi, 0) and s == 0:
                            continue
                        if is_group(gi, 0) and s == 1:
                            nc.gpsimd.tensor_tensor(sums[i][:], probs[0][:], probs[1][:], ALU.add).then_inc(summed, 2)
                        else:
                            pool.wait_ge(summed, t + GROUP)
                            nc.gpsimd.tensor_tensor(sums[i][:], sums[i][:], probs[s][:], ALU.add).then_inc(summed, 1)
                each_group(pool, group)
            each_block(pool, run)

        @block.vector
        def _(dve):
            dve.sem_inc(max_ready, 1)
            dve.sem_inc(side_free, 1)
            dve.sem_inc(y_ready, 2)

            def chunk_max(use, c):
                dve.wait_ge(side_full, use + 1)
                nc.vector.reduce_max(part_max[:, c:c + 1], side[c % 2][:], AX.X).then_inc(side_free, 1)

            def tile_max(use):
                dve.wait_ge(side_free, use + 2)
                nc.vector.tensor_reduce(pm_max[:, 0:1], part_max[:], AX.X, ALU.max)
                nc.vector.tensor_reduce(pm_max[:, 1:2], part_max[:], AX.X, ALU.max, negate=True).then_inc(max_ready, 1)

            def shift(use, tile, i, gi):
                dve.wait_ge(side_full, use + 1)
                nc.vector.tensor_copy(row[:], side[1][0:2, 0:P]).then_inc(side_free, 1)
                dve.wait_ge(side_free, use + 2)
                nc.vector.tensor_copy(row_high[:], row[:]).then_inc(row_step, 1)
                dve.wait_ge(row_step, tile + 1)
                nc.vector.scalar_tensor_tensor(g_cols[i][R:KR, bass.ds(gi * P, P)], row[:], p.low_2[:],
                                               plain(row_high[:]), ALU.mult, ALU.subtract).then_inc(shift_ready, 1)

            with dve.Fori(0, GROUPS) as tile:
                for c in range(2 * GROUP):
                    chunk_max(tile * TILE_USES + c, c)
                tile_max(tile * TILE_USES + 2 * GROUP - 1)
                shift(tile * TILE_USES + 2 * GROUP, tile, 0, tile)

            def run(k, i, pair):
                use = first_use(k)
                if not is_from(k, BLOCKS - 1):
                    def group(gi, slot, filling):
                        first = use + gi * TILE_USES
                        if not is_group(gi, 0):
                            shift(first - 1, (k + 1) * GROUPS + gi - 1, 1 - i, gi - 1)
                        for c in range(2 * GROUP):
                            chunk_max(first + c, c)
                        tile_max(first + 2 * GROUP - 1)
                    each_group(dve, group)
                    shift(use + GROUPS * TILE_USES - 1, (k + 2) * GROUPS - 1, 1 - i, GROUPS - 1)
                    use = use + GROUPS * TILE_USES
                for h in range(HALVES):
                    dve.wait_ge(side_full, use + h + 1)
                    nc.vector.reciprocal(inv[:, h * BANK:(h + 1) * BANK], side[h][:]).then_inc(side_free, 1)
                dve.wait_ge(side_free, use + HALVES + 1)
                dve.wait_ge(att_copied, k + 1)
                dve.wait_ge(y_stored[i], DMA * pair)
                nc.vector.tensor_tensor(y_out[i][:], att_sb[i][:], inv[:], ALU.mult).then_inc(norm_step, 1)
                dve.wait_ge(norm_step, k + 1)
                dve.wait_ge(x_res_loaded[i], DMA * (pair + 1))
                nc.vector.scalar_tensor_tensor(y_out[i][:], y_out[i][:], p.gamma[:], x_res[i][:],
                                               ALU.mult, ALU.add).then_inc(y_ready, 1)
            each_block(dve, run)


def prefix(p):
    nc, B, N, C, H = p.nc, p.B, p.N, p.C, p.HEADS
    D = C
    TILES = 4
    G = TILES * P
    GROUPS = N // G
    FILLS = GROUPS // 2
    KV = H * D
    ROWS = PARTS * H
    W = P + H
    HALF = H // 2
    EPS = 1e-5
    assert G == BANK and HALF * P == BANK
    with ExitStack() as ctx:
        sb = lambda n, s, dt=F32: ctx.enter_context(nc.sbuf_tensor(n, s, dt))
        ps = lambda n, s: ctx.enter_context(nc.psum_tensor(n, s, F32))
        pair = lambda n, s, dt=F32: [sb(f"{n}{i}", s, dt) for i in range(2)]
        w_high, w_low = sb("w_high", [C, 2 * KV], F32R), sb("w_low", [C, 2 * KV], F32R)
        q_all = sb("q_all", [P, KV])
        tri = sb("tri", [P, P])
        eye = sb("eye", [P, H, H])
        low_e, low_r = sb("low_e", [ROWS, 1]), sb("low_r", [ROWS, 1])
        sign_r = sb("sign_r", [ROWS, 1])
        own = sb("own", [ROWS, H])
        ones_row = sb("ones_row", [ROWS, G])
        minus_half = sb("minus_half", [P, TILES])
        y_in, y_res, t2_sb = pair("y_in", [P, TILES, C]), pair("y_res", [P, TILES, C]), pair("t2_sb", [P, TILES, C])
        stats = sb("stats", [P, TILES, 6])
        both, differ, spread, mean, var = (sb(x, [P, TILES]) for x in ("both", "differ", "spread", "mean", "var"))
        rstd = sb("rstd", [P, TILES])
        tn = sb("tn", [P, TILES, C])
        tn_high, tn_low = sb("tn_high", [C, G], F32R), sb("tn_low", [C, G], F32R)
        k_sb, kq = pair("k_sb", [P, KV]), pair("kq", [P, KV])
        v_sb = pair("v_sb", [P, TILES, KV])
        s_tok = sb("s_tok", [P, TILES, H])
        s_rep = sb("s_rep", [P, TILES, PARTS, H])
        s_row = sb("s_row", [ROWS, G])
        m_row, u_row = pair("m_row", [ROWS, G]), pair("u_row", [ROWS, G])
        less = sb("less", [ROWS, G])
        e_row, r_row = pair("e_row", [ROWS, G]), pair("r_row", [ROWS, G])
        e_high, r_high = sb("e_high", [ROWS, G], F32R), sb("r_high", [ROWS, G], F32R)
        inv_u = sb("inv_u", [ROWS, G])
        e_parts = pair("e_parts", [ROWS, G], F32R)
        r_parts = sb("r_parts", [ROWS, G], F32R)
        r_heads = pair("r_heads", [ROWS, H, G], F32R)
        e_tok = sb("e_tok", [P, TILES, H])
        mat = pair("mat", [P, H, W])
        w_sum = sb("w_sum", [D, H])
        w_turned = sb("w_turned", [H, D])
        o_sb = sb("o_sb", [D, P])
        k_ps, v_ps = ps("k_ps", [P, KV]), ps("v_ps", [P, KV])
        a_ps = [ps(f"a_ps{i}", [P, HALF, P]) for i in range(2)]
        o_ps = ps("o_ps", [P, BANK])
        misc = ps("misc", [P, BANK])

        prefix_constants(p, locals())

        names = ("stats_made rstd_made tn_made tn_turned tn_high_made tn_low_made k_made k_taken v_made v_taken "
                 "kq_made s_made s_repeated s_turned s_row_made less_made e_made r_parts_made r_heads_made "
                 "e_turned e_tok_made a_made mat_made o_made w_added w_turn w_turned_made o_taken o_turned t2_made "
                 "was_reset step").split()
        S = {n: p.sem("px_" + n) for n in names}
        y_in_loaded = [p.sem(f"y_in_loaded{i}") for i in range(2)]
        y_res_loaded = [p.sem(f"y_res_loaded{i}") for i in range(2)]
        t2_stored = [p.sem(f"t2_stored{i}") for i in range(2)]
        CREDITS = {"tn_made": 2, "t2_made": 2 * TILES, "k_taken": 1, "v_taken": 1, "kq_made": 2, "s_made": 2}
        t2_v = p.t2_d
        block = ctx.enter_context(nc.Block())

        def wait(engine, name, count):
            engine.wait_ge(S[name], count + CREDITS.get(name, 0))

        def each(engine, run, drain):
            with engine.Fori(0, B) as b:
                run(b, 0, 0, 0)
                with engine.Fori(0, FILLS - 1) as g2:
                    run(b, 2 * g2 + 1, 1, g2)
                    run(b, 2 * g2 + 2, 0, g2 + 1)
                run(b, GROUPS - 1, 1, FILLS - 1)
                drain(b)

        def is_group(g, which):
            return isinstance(g, int) and g == which

        @block.sync
        def _(sp):
            def rows_of(dram, first):
                return dram[bass.ds(first, G), :].rearrange("(t p) c -> p t c", p=P)

            def load_in(b, g, i):
                n = b * GROUPS + g
                at = sp.snap(n * G)
                wait(sp, "tn_made", n - 1)
                sp.dma_start(y_in[i][:], rows_of(p.y_tok, at)).then_inc(y_in_loaded[i], DMA)

            def load_res(b, g, i):
                n = b * GROUPS + g
                at = sp.snap(n * G)
                wait(sp, "t2_made", (n - 1) * TILES)
                sp.dma_start(y_res[i][:], rows_of(p.y_tok, at)).then_inc(y_res_loaded[i], DMA)

            def store(b, g, i):
                n = b * GROUPS + g
                at = sp.snap(n * G)
                wait(sp, "t2_made", (n + 1) * TILES)
                sp.dma_start(rows_of(p.t2_d, at), t2_sb[i][:]).then_inc(t2_stored[i], DMA)

            def run(b, g, i, filling):
                if is_group(g, 0):
                    load_in(b, 0, 0)
                if not is_group(g, GROUPS - 1):
                    load_in(b, g + 1, 1 - i)
                load_res(b, g, i)
                if not is_group(g, 0):
                    store(b, g - 1, 1 - i)
            each(sp, run, lambda b: store(b, GROUPS - 1, 1))
            for i in range(2):
                sp.wait_ge(t2_stored[i], (B * FILLS + 1) * DMA)

        @block.tensor
        def _(pe):
            def keys_values(n, tt):
                t = n * TILES + tt
                cols = slice(tt * P, (tt + 1) * P)
                passes = ((tn_high, w_high), (tn_low, w_high), (tn_high, w_low))
                for made, taken, out, first in (("k_made", "k_taken", k_ps, 0), ("v_made", "v_taken", v_ps, KV)):
                    wait(pe, taken, t)
                    for h in range(KV // BANK):
                        for j, (x, w) in enumerate(passes):
                            done = nc.tensor.matmul(out[:, h * BANK:(h + 1) * BANK], x[:, cols],
                                                    w[:, first + h * BANK:first + (h + 1) * BANK],
                                                    start=j == 0, stop=j == len(passes) - 1)
                    done.then_inc(S[made], 1)

            def matrices(f, i, tt):
                t = f * TILES + tt
                cols = slice(tt * P, (tt + 1) * P)
                wait(pe, "r_heads_made", t + 1)
                for half in range(2):
                    nc.tensor.matmul(a_ps[half][:], e_parts[i][:, cols], r_heads[i][:, half * HALF:(half + 1) * HALF, cols],
                                     start=True, stop=True).then_inc(S["a_made"], 1)

            def weigh(b, f, i, tt, first_of_image):
                t = f * TILES + tt
                wait(pe, "mat_made", t + 1)
                for h in range(H):
                    nc.tensor.matmul(o_ps[:, 0:W], v_sb[i][:, tt, h * D:(h + 1) * D], mat[tt % 2][:, h, :],
                                     start=h == 0, stop=False)
                if first_of_image and tt == 0:
                    wait(pe, "was_reset", b + 1)
                else:
                    wait(pe, "w_turned_made", t)
                nc.tensor.matmul(o_ps[:, 0:P], w_turned[:], r_row[i][0:H, tt * P:(tt + 1) * P],
                                 start=False, stop=True).then_inc(S["o_made"], 1)

            def turn(f, tt, before):
                t = f * TILES + tt
                wait(pe, *before)
                wait(pe, "w_added", t + 1)
                nc.tensor.transpose(misc[0:H, 0:D], w_sum[:], p.ident[:]).then_inc(S["w_turn"], 1)
                wait(pe, "w_turned_made", t + 1)
                wait(pe, "o_taken", t + 1)
                nc.tensor.transpose(misc[:, 0:P], o_sb[:], p.ident[:]).then_inc(S["o_turned"], 1)

            def turn_e(i):
                for tt in range(TILES):
                    done = nc.tensor.transpose(misc[:, tt * H:(tt + 1) * H], e_row[i][0:H, tt * P:(tt + 1) * P],
                                               p.ident[0:H, 0:H])
                done.then_inc(S["e_turned"], 1)

            def run(b, g, i, filling):
                n = b * GROUPS + g
                f = n - 1
                alone = is_group(g, 0)
                wait(pe, "t2_made", n * TILES if alone else f * TILES)
                wait(pe, "tn_made", n + 1)
                for tt in range(TILES):
                    done = nc.tensor.transpose(misc[:, tt * P:(tt + 1) * P], tn[:, tt, :], p.ident[:])
                done.then_inc(S["tn_turned"], 1)
                wait(pe, "tn_low_made", n + 1)
                keys_values(n, 0)
                keys_values(n, 1)
                if not alone:
                    matrices(f, 1 - i, 0)
                    turn_e(1 - i)
                keys_values(n, 2)
                if not alone:
                    weigh(b, f, 1 - i, 0, is_group(g, 1) or not isinstance(g, int) and i == 1)
                    matrices(f, 1 - i, 1)
                    turn(f, 0, ("e_tok_made", n))
                keys_values(n, 3)
                if not alone:
                    for tt in (1, 2):
                        weigh(b, f, 1 - i, tt, False)
                        matrices(f, 1 - i, tt + 1)
                        turn(f, tt, ("t2_made", f * TILES + tt))
                wait(pe, "s_repeated", n + 1)
                if not alone:
                    wait(pe, "t2_made", f * TILES + 3)
                for tt in range(TILES):
                    done = nc.tensor.transpose(misc[0:ROWS, tt * P:(tt + 1) * P], s_rep[:, tt], p.ident[:])
                done.then_inc(S["s_turned"], 1)
                if not alone:
                    weigh(b, f, 1 - i, 3, False)
                    turn(f, 3, ("s_row_made", n + 1))

            def drain(b):
                f = b * GROUPS + GROUPS - 1
                wait(pe, "t2_made", f * TILES)
                matrices(f, 1, 0)
                turn_e(1)
                for tt in range(TILES):
                    weigh(b, f, 1, tt, False)
                    if tt < TILES - 1:
                        matrices(f, 1, tt + 1)
                    turn(f, tt, ("t2_made", f * TILES + tt) if tt else ("e_tok_made", f + 1))
            each(pe, run, drain)

        @block.scalar
        def _(act):
            act.sem_inc(S["k_taken"], 1)
            act.sem_inc(S["v_taken"], 1)

            def silu(n, i, tt):
                t = n * TILES + tt
                wait(act, "k_made", t + 1)
                wait(act, "kq_made", t - 1)
                nc.scalar.activation(k_sb[tt % 2][:], k_ps[:], ACT.Silu).then_inc(S["k_taken"], 1)
                wait(act, "v_made", t + 1)
                nc.scalar.activation(v_sb[i][:, tt, :], v_ps[:], ACT.Silu).then_inc(S["v_taken"], 1)

            def take(f, tt):
                t = f * TILES + tt
                wait(act, "w_added", t + 1)
                nc.scalar.copy(o_sb[:], o_ps[:, 0:P]).then_inc(S["o_taken"], 1)
                wait(act, "w_turn", t + 1)
                nc.scalar.copy(w_turned[:], misc[0:H, 0:D]).then_inc(S["w_turned_made"], 1)

            def run(b, g, i, filling):
                n = b * GROUPS + g
                f = n - 1
                alone = is_group(g, 0)
                wait(act, "tn_turned", n + 1)
                nc.scalar.copy(tn_high[:], misc[:]).then_inc(S["tn_high_made"], 1)
                for tt in range(TILES):
                    silu(n, i, tt)
                    if not alone and tt >= 2:
                        take(f, tt - 2)
                if not alone:
                    take(f, 2)
                wait(act, "s_turned", n + 1)
                nc.scalar.copy(s_row[:], misc[0:ROWS, :]).then_inc(S["s_row_made"], 1)
                if not alone:
                    take(f, 3)
                wait(act, "less_made", n + 1)
                nc.scalar.activation(e_row[i][:], less[:], ACT.Exp).then_inc(S["e_made"], 1)

            def drain(b):
                for tt in range(TILES):
                    take(b * GROUPS + GROUPS - 1, tt)
            each(act, run, drain)

        @block.gpsimd
        def _(pool):
            pool.sem_inc(S["kq_made"], 2)

            def inverse_deviation(n):
                wait(pool, "stats_made", n + 1)
                nc.gpsimd.tensor_tensor(rstd[:], var[:], minus_half[:], ALU.pow).then_inc(S["rstd_made"], 1)

            def run(b, g, i, filling):
                n = b * GROUPS + g
                if is_group(g, 0):
                    inverse_deviation(n)
                for tt in range(TILES):
                    t = n * TILES + tt
                    wait(pool, "k_taken", t + 1)
                    wait(pool, "s_made", t - 1)
                    nc.gpsimd.tensor_tensor(kq[tt % 2][:], k_sb[tt % 2][:], q_all[:], ALU.mult).then_inc(S["kq_made"], 1)
                if not is_group(g, GROUPS - 1):
                    inverse_deviation(n + 1)
                wait(pool, "r_parts_made", n + 1)
                for tt in range(TILES):
                    cols = slice(tt * P, (tt + 1) * P)
                    nc.gpsimd.tensor_tensor(r_heads[i][:, :, cols],
                                            plain(r_parts[:, cols]).unsqueeze(1).to_broadcast([ROWS, H, P]),
                                            own[:].unsqueeze(2).to_broadcast([ROWS, H, P]), ALU.mult).then_inc(S["r_heads_made"], 1)
            each(pool, run, lambda b: None)

        @block.vector
        def _(dve):
            for name in ("tn_made", "t2_made", "s_made"):
                dve.sem_inc(S[name], CREDITS[name])
            for i in range(2):
                dve.sem_inc(t2_stored[i], DMA)
            steps = [0]

            def step(instruction, total):
                instruction.then_inc(S["step"], 1)
                dve.wait_ge(S["step"], total)

            PER_GROUP = 9
            PER_IMAGE = GROUPS * PER_GROUP

            def normalise(b, g, i, filling, base):
                n = b * GROUPS + g
                dve.wait_ge(y_in_loaded[i], (b * FILLS + filling + 1) * DMA)
                for tt in range(TILES):
                    done = nc.vector.bn_stats(stats[:, tt, :], y_in[i][:, tt, :])
                step(done, base + 1)
                variance(dve, nc, stats, both, differ, spread, mean, var, C, EPS, lambda x, k: step(x, base + 1 + k)).then_inc(S["stats_made"], 1)
                wait(dve, "rstd_made", n + 1)
                for tt in range(TILES):
                    done = nc.vector.tensor_scalar(tn[:, tt, :], y_in[i][:, tt, :], mean[:, tt:tt + 1], rstd[:, tt:tt + 1],
                                                   ALU.subtract, ALU.mult)
                done.then_inc(S["tn_made"], 1)

            def sum_heads(n, tt):
                t = n * TILES + tt
                wait(dve, "kq_made", t + 1)
                nc.vector.tensor_reduce(s_tok[:, tt, :], kq[tt % 2][:].rearrange("p (h d) -> p h d", d=D), AX.X,
                                        ALU.add).then_inc(S["s_made"], 1)

            def mask(f, tt):
                t = f * TILES + tt
                nc.vector.tensor_tensor(mat[tt % 2][:, :, P:W], e_tok[:, tt, :].unsqueeze(2).to_broadcast([P, H, H]),
                                        eye[:], ALU.mult)
                for half in range(2):
                    wait(dve, "a_made", 2 * t + half + 1)
                    done = nc.vector.tensor_tensor(mat[tt % 2][:, half * HALF:(half + 1) * HALF, 0:P], a_ps[half][:],
                                                   tri[:].unsqueeze(1).to_broadcast([P, HALF, P]), ALU.mult)
                done.then_inc(S["mat_made"], 1)

            def add_w(f, tt):
                t = f * TILES + tt
                wait(dve, "o_made", t + 1)
                nc.vector.tensor_tensor(w_sum[:], w_sum[:], o_ps[:, P:W], ALU.add).then_inc(S["w_added"], 1)

            def residual(f, i, tt, b=None, filling=None):
                t = f * TILES + tt
                wait(dve, "o_turned", t + 1)
                if tt == 0:
                    dve.wait_ge(y_res_loaded[i], (b * FILLS + filling + 1) * DMA)
                    dve.wait_ge(t2_stored[i], (b * FILLS + filling + 1) * DMA)
                nc.vector.tensor_tensor(t2_sb[i][:, tt, :], misc[:, 0:P], y_res[i][:, tt, :], ALU.add).then_inc(S["t2_made"], 1)

            def copy_e(f):
                wait(dve, "e_turned", f + 1)
                nc.vector.tensor_copy(e_tok[:].rearrange("p t h -> p (t h)"), misc[:, 0:TILES * H]).then_inc(S["e_tok_made"], 1)
                wait(dve, "e_tok_made", f + 1)

            def run(b, g, i, filling):
                n = b * GROUPS + g
                f = n - 1
                base = b * PER_IMAGE + g * PER_GROUP + 4
                alone = is_group(g, 0)
                before = filling - (1 if i == 0 else 0)
                if alone:
                    wait(dve, "t2_made", n * TILES)
                    nc.vector.memset(w_sum[:], 0.0)
                    nc.vector.memset(w_turned[:], 0.0).then_inc(S["was_reset"], 1)
                    normalise(b, 0, 0, 0, b * PER_IMAGE)
                wait(dve, "tn_high_made", n + 1)
                nc.vector.tensor_tensor(tn_low[:], misc[:], plain(tn_high[:]), ALU.subtract).then_inc(S["tn_low_made"], 1)
                sum_heads(n, 0)
                if not alone:
                    copy_e(f)
                    mask(f, 0)
                sum_heads(n, 1)
                for tt in range(2):
                    if not alone:
                        add_w(f, tt)
                        mask(f, tt + 1)
                        residual(f, 1 - i, tt, b, before)
                    sum_heads(n, tt + 2)
                wait(dve, "s_made", (n + 1) * TILES)
                nc.vector.tensor_copy(s_rep[:], s_tok[:].unsqueeze(2).to_broadcast([P, TILES, PARTS, H])).then_inc(S["s_repeated"], 1)
                if not alone:
                    add_w(f, 2)
                    mask(f, 3)
                    residual(f, 1 - i, 2)
                    add_w(f, 3)
                    residual(f, 1 - i, 3)
                wait(dve, "s_row_made", n + 1)
                step(nc.vector.tensor_tensor_scan(m_row[i][:], s_row[:], s_row[:], -3.0e38 if alone else m_row[1 - i][:, G - 1:G],
                                                  ALU.max, ALU.max), base + 1)
                nc.vector.tensor_tensor(less[:], s_row[:], m_row[i][:], ALU.subtract).then_inc(S["less_made"], 1)
                if not is_group(g, GROUPS - 1):
                    normalise(b, g + 1, 1 - i, filling + (1 if i == 1 else 0), base + 1)
                    base = base + 4
                wait(dve, "e_made", n + 1)
                after = [0]

                def chain(instruction):
                    after[0] += 1
                    step(instruction, base + 1 + after[0])
                nc.vector.tensor_copy(e_high[:], e_row[i][:])
                chain(nc.vector.tensor_tensor_scan(u_row[i][:], ones_row[:], e_row[i][:], 0.0 if alone else u_row[1 - i][:, G - 1:G],
                                                   ALU.mult, ALU.add))
                nc.vector.scalar_tensor_tensor(e_parts[i][:], e_row[i][:], low_e[:], plain(e_high[:]), ALU.mult, ALU.subtract)
                chain(nc.vector.reciprocal(inv_u[:], u_row[i][:]))
                chain(nc.vector.tensor_scalar(r_row[i][:], inv_u[:], sign_r[:], None, ALU.mult))
                chain(nc.vector.tensor_copy(r_high[:], r_row[i][:]))
                nc.vector.scalar_tensor_tensor(r_parts[:], r_row[i][:], low_r[:], plain(r_high[:]), ALU.mult,
                                               ALU.subtract).then_inc(S["r_parts_made"], 1)

            def drain(b):
                f = b * GROUPS + GROUPS - 1
                copy_e(f)
                mask(f, 0)
                for tt in range(TILES):
                    add_w(f, tt)
                    if tt < TILES - 1:
                        mask(f, tt + 1)
                    residual(f, 1, tt, b, FILLS - 1)
            each(dve, run, drain)


def variance(dve, nc, stats, both, differ, spread, mean, var, width, eps, step):
    nc.vector.tensor_tensor(both[:], stats[:, :, 1], stats[:, :, 4], ALU.add)
    nc.vector.tensor_tensor(spread[:], stats[:, :, 2], stats[:, :, 5], ALU.add)
    step(nc.vector.tensor_tensor(differ[:], stats[:, :, 1], stats[:, :, 4], ALU.subtract), 1)
    step(nc.vector.tensor_tensor(differ[:], differ[:], differ[:], ALU.mult), 2)
    nc.vector.tensor_scalar(mean[:], both[:], 0.5, None, ALU.mult)
    step(nc.vector.tensor_scalar(differ[:], differ[:], 0.25, eps, ALU.mult, ALU.add), 3)
    return nc.vector.scalar_tensor_tensor(var[:], spread[:], 1.0 / width, differ[:], ALU.mult, ALU.add)


def prefix_constants(p, v):
    nc, H, C = p.nc, p.HEADS, p.C
    KV = H * C
    WT = 2 * KV // P
    ROWS = PARTS * H
    w_in, q_all, k_ps, v_ps = v["y_in"], v["q_all"], v["k_ps"], v["v_ps"]
    TILES = v["TILES"]
    LOADS = WT // TILES
    loaded = [p.sem(f"wkv_loaded{i}") for i in range(2)]
    q_loaded = p.sem("q_loaded")
    turned, rounded, split = p.sem("wkv_turned"), p.sem("wkv_rounded"), p.sem("wkv_split")
    filled, chosen, stepped = p.sem("pc_filled"), p.sem("pc_chosen"), p.sem("pc_stepped")
    rows = p.ins["L1_attn_W_kv"].rearrange("(n t p) c -> n p t c", p=P, t=TILES)
    banks = (k_ps, v_ps)
    tri, eye, own = v["tri"], v["eye"], v["own"]
    bands = v["less"]

    def parts(tensor, j):
        return tensor[:].rearrange("c (s h d) -> c s (h d)", s=2, d=C)[:, :, j * (TILES * P // 2):(j + 1) * (TILES * P // 2)]

    with nc.Block() as block:
        @block.sync
        def _(sp):
            sp.dma_start(q_all[:], p.ins["L1_attn_q_proj"].rearrange("h d -> (h d)").partition_broadcast(P)).then_inc(q_loaded, DMA)
            for j in range(LOADS):
                if j >= 2:
                    sp.wait_ge(turned, j - 1)
                sp.dma_start(w_in[j % 2][:], rows[j]).then_inc(loaded[j % 2], DMA)
            sp.wait_ge(q_loaded, DMA)

        @block.tensor
        def _(pe):
            for j in range(LOADS):
                pe.wait_ge(loaded[j % 2], DMA * (j // 2 + 1))
                if j >= 2:
                    pe.wait_ge(split, j - 1)
                for t in range(TILES):
                    done = nc.tensor.transpose(banks[j % 2][:, t * P:(t + 1) * P], w_in[j % 2][:, t, :], p.ident[:])
                done.then_inc(turned, 1)

        @block.vector
        def _(dve):
            for j in range(LOADS):
                source = banks[j % 2][:, 0:BANK].rearrange("c (x s) -> c s x", s=2)
                dve.wait_ge(turned, j + 1)
                nc.vector.tensor_copy(parts(v["w_high"], j), source).then_inc(rounded, 1)
                dve.wait_ge(rounded, j + 1)
                nc.vector.tensor_tensor(parts(v["w_low"], j), source, plain(parts(v["w_high"], j)),
                                        ALU.subtract).then_inc(split, 1)
            dve.wait_ge(chosen, 5)
            nc.vector.memset(v["ones_row"][:], 1.0)
            nc.vector.memset(v["minus_half"][:], -0.5)
            nc.vector.tensor_copy(v["low_e"][:], bands[:, 1:2])
            nc.vector.tensor_tensor(v["low_r"][:], bands[:, 0:1], bands[:, 1:2], ALU.subtract).then_inc(stepped, 1)
            dve.wait_ge(stepped, 1)
            nc.vector.tensor_tensor(v["low_r"][:], v["low_r"][:], bands[:, 2:3], ALU.add)
            nc.vector.tensor_tensor(v["sign_r"][:], bands[:, 2:3], bands[:, 0:1], ALU.subtract).then_inc(stepped, 1)
            dve.wait_ge(stepped, 2)
            nc.vector.tensor_scalar(v["sign_r"][:], v["sign_r"][:], 2.0 / H, 1.0 / H, ALU.mult, ALU.add)
            nc.vector.tensor_tensor(own[:], bands[:, 8:8 + H], bands[:, 8 + H:8 + 2 * H], ALU.add).then_inc(stepped, 1)
            spare = bands[:, 8 + PARTS * H:8 + (PARTS + 1) * H]
            nc.vector.tensor_tensor(spare, bands[:, 8 + 2 * H:8 + 3 * H], bands[:, 8 + 3 * H:8 + 4 * H],
                                    ALU.add).then_inc(stepped, 1)
            dve.wait_ge(stepped, 4)
            nc.vector.tensor_tensor(own[:], own[:], spare, ALU.add)

        @block.gpsimd
        def _(pool):
            nc.gpsimd.memset(tri[:], 1.0).then_inc(filled, 1)
            nc.gpsimd.memset(eye[:], 0.0).then_inc(filled, 1)
            nc.gpsimd.memset(bands[:, 0:8], 1.0).then_inc(filled, 1)
            nc.gpsimd.memset(bands[:, 8:8 + PARTS * H], 0.0).then_inc(filled, 1)
            pool.wait_ge(filled, 4)
            nc.gpsimd.affine_select(out=tri[:], in_=tri[:], compare_op=ALU.is_ge, fill=0.0, base=0,
                                    pattern=[[1, P]], channel_multiplier=-1).then_inc(chosen, 1)
            nc.gpsimd.affine_select(out=eye[:], in_=eye[:], compare_op=ALU.not_equal, fill=1.0, base=0,
                                    pattern=[[1, H], [-1, H]], channel_multiplier=0).then_inc(chosen, 1)
            nc.gpsimd.affine_select(out=bands[:, 0:3], in_=bands[:, 0:3], compare_op=ALU.is_ge, fill=0.0, base=-H,
                                    pattern=[[-H, 3]], channel_multiplier=1).then_inc(chosen, 1)
            nc.gpsimd.affine_select(out=bands[:, 8:8 + PARTS * H], in_=bands[:, 8:8 + PARTS * H],
                                    compare_op=ALU.not_equal, fill=1.0, base=0,
                                    pattern=[[-1, PARTS * H]], channel_multiplier=1).then_inc(chosen, 2)


def choose(p):
    nc, B, N, C, E = p.nc, p.B, p.N, p.C, p.E
    TILES = 4
    G = TILES * P
    GROUPS = N // G
    K = 8
    TAKEN = -3.0e38
    EPS = 1e-5
    p.pooled = p.const("pooled", [C, E, B])
    with ExitStack() as ctx:
        sb = lambda n, s, dt=F32: ctx.enter_context(nc.sbuf_tensor(n, s, dt))
        ps = lambda n, s: ctx.enter_context(nc.psum_tensor(n, s, F32))
        pair = lambda n, s, dt=F32: [sb(f"{n}{i}", s, dt) for i in range(2)]
        gate_in, gate_w, gate_b = sb("gate_in", [E, C]), sb("gate_w", [C, E]), sb("gate_b", [E, 1])
        t_in = pair("t_in", [P, TILES, C])
        stats = pair("c_stats", [P, TILES, 6])
        both, differ, spread, mean, var, rstd, minus_half = (
            sb("c_" + x, [P, TILES]) for x in ("both", "differ", "spread", "mean", "var", "rstd", "minus_half"))
        tn = sb("c_tn", [P, p.NT, C])
        tn_group = pair("c_tn_group", [P, TILES, C])
        zeros = sb("c_zeros", [P, P])
        tn_turned = pair("c_tn_turned", [C, G])
        logits, left, probs = sb("logits", [E, N]), sb("left", [E, N]), sb("c_probs", [E, N])
        top = sb("top", [E, K])
        minus_top, total, scale = sb("minus_top", [E, 1]), sb("total", [E, 1]), sb("scale", [E, 1])
        weights = pair("weights", [E, G])
        weights_tok = pair("weights_tok", [P, TILES, E])
        pooled_sb = sb("pooled_sb", [E, C])
        turn_ps = [ps(f"turn_ps{i}", [P, G]) for i in range(2)]
        gate_ps = [ps(f"gate_ps{i}", [P, G]) for i in range(2)]
        w_ps = [ps(f"w_ps{i}", [P, TILES, E]) for i in range(2)]
        pool_ps = ps("pool_ps", [E, C])
        pooled_ps = ps("pooled_ps", [C, E])

        names = ("loaded gate_turned gate_ready filled stats_made rstd_made tn_made turned copied gated logits_made "
                 "maxed topped replaced exped scaled masked kept weights_made w_turned w_copied pooled pool_copied pool_turned "
                 "pooled_made step").split()
        S = {n: p.sem("ch_" + n) for n in names}
        t_loaded = [p.sem(f"t_loaded{i}") for i in range(2)]
        w_stored = [p.sem(f"w_stored{i}") for i in range(2)]
        CREDITS = {"tn_made": 2, "copied": 2, "logits_made": 2, "turned": 2, "w_copied": 2, "pooled_made": 1, "pooled": 1, "w_turned": 2}
        block = ctx.enter_context(nc.Block())

        def at(name, count):
            return S[name], count + CREDITS.get(name, 0)

        def wait(engine, name, count):
            engine.wait_ge(*at(name, count))

        def credit(engine, *which):
            for name in which:
                engine.sem_inc(S[name], CREDITS[name])

        def groups(engine, run):
            with engine.Fori(0, GROUPS // 2) as g2:
                for i in range(2):
                    run(2 * g2 + i, i, g2)

        @block.sync
        def _(sp):
            sp.dma_start(gate_in[:], p.ins["L1_ffn_gate_w"]).then_inc(S["loaded"], DMA)
            sp.dma_start(gate_b[:], p.ins["L1_ffn_gate_b"].rearrange("(e o) -> e o", o=1)).then_inc(S["loaded"], DMA)
            with sp.Fori(0, B * GROUPS // 2) as n2:
                for i in range(2):
                    n = 2 * n2 + i
                    at = sp.snap(n * G)
                    wait(sp, "tn_made", n - 1)
                    sp.dma_start(t_in[i][:], p.t2_d[bass.ds(at, G), :].rearrange("(t p) c -> p t c", p=P)).then_inc(t_loaded[i], DMA)

        @block.tensor
        def _(pe):
            pe.wait_ge(S["loaded"], 2 * DMA)
            nc.tensor.transpose(pooled_ps[:], gate_in[:], p.ident[0:E, 0:E]).then_inc(S["gate_turned"], 1)
            pe.wait_ge(S["gate_ready"], 1)
            credit(pe, "turned", "pooled", "w_turned")
            with pe.Fori(0, B) as b:
                def gate(g, i, filling):
                    n = b * GROUPS + g
                    wait(pe, "copied", n - 1)
                    wait(pe, "tn_made", n + 1)
                    for tt in range(TILES):
                        done = nc.tensor.transpose(turn_ps[i][:, tt * P:(tt + 1) * P], tn_group[i][:, tt, :], p.ident[:])
                    done.then_inc(S["turned"], 1)
                    wait(pe, "copied", n + 1)
                    wait(pe, "logits_made", n - 1)
                    nc.tensor.matmul(gate_ps[i][0:E, :], gate_w[:], tn_turned[i][:], start=True, stop=True).then_inc(S["gated"], 1)
                groups(pe, gate)

                def pool(g, i, filling):
                    n = b * GROUPS + g
                    wait_first(pe, S["gate_ready"], at("w_copied", n - 1), at("weights_made", n + 1))
                    for tt in range(TILES):
                        done = nc.tensor.transpose(w_ps[i][:, tt, :], weights[i][:, tt * P:(tt + 1) * P], p.ident[0:E, 0:E])
                    done.then_inc(S["w_turned"], 1)
                    wait_first(pe, S["gate_ready"], at("w_copied", n + 1))
                    for tt in range(TILES):
                        done = nc.tensor.matmul(pool_ps[:], weights_tok[i][:, tt, :], tn[:, bass.ds(g * TILES + tt, 1), :],
                                                start=False, stop=False, skip_group_check=True)
                    return done
                wait(pe, "pooled_made", b)
                nc.tensor.matmul(pool_ps[:], zeros[:, 0:E], p.ident[:], start=True, stop=False, skip_group_check=True)
                groups(pe, pool)
                nc.tensor.matmul(pool_ps[:], zeros[:, 0:E], p.ident[:], start=False, stop=True, skip_group_check=True).then_inc(S["pooled"], 1)
                wait_first(pe, S["gate_ready"], at("pool_copied", b + 1))
                nc.tensor.transpose(pooled_ps[:], pooled_sb[:], p.ident[0:E, 0:E]).then_inc(S["pool_turned"], 1)

        @block.scalar
        def _(act):
            credit(act, "copied", "logits_made", "w_copied")
            act.wait_ge(S["gate_turned"], 1)
            nc.scalar.copy(gate_w[:], pooled_ps[:]).then_inc(S["gate_ready"], 1)
            with act.Fori(0, B) as b:
                def gate(g, i, filling):
                    n = b * GROUPS + g
                    wait(act, "turned", n + 1)
                    wait(act, "gated", n - 1 + 2)
                    nc.scalar.copy(tn_turned[i][:], turn_ps[i][:]).then_inc(S["copied"], 1)
                    wait(act, "gated", n + 1 + 2)
                    nc.scalar.activation(logits[:, bass.ds(g * G, G)], gate_ps[i][0:E, :], ACT.Identity,
                                         bias=gate_b[:]).then_inc(S["logits_made"], 1)
                groups(act, gate)
                wait(act, "topped", b + 1)
                nc.scalar.activation(probs[:], logits[:], ACT.Exp, bias=minus_top[:], accum_out=total[:]).then_inc(S["exped"], 1)

                def pool(g, i, filling):
                    n = b * GROUPS + g
                    wait(act, "w_turned", n + 1)
                    nc.scalar.copy(weights_tok[i][:], w_ps[i][:]).then_inc(S["w_copied"], 1)
                    wait(act, "weights_made", n + 1)
                    act.dma_start(p.chosen_d[:, bass.ds(b * N + g * G, G)], weights[i][:]).then_inc(w_stored[i], DMA)
                groups(act, pool)
                wait(act, "pooled", b + 1)
                nc.scalar.copy(pooled_sb[:], pool_ps[:]).then_inc(S["pool_copied"], 1)
            for i in range(2):
                act.wait_ge(w_stored[i], (B * (GROUPS // 2) + 1) * DMA)

        @block.gpsimd
        def _(pool):
            with pool.Fori(0, B * GROUPS) as n:
                wait(pool, "stats_made", n + 1)
                nc.gpsimd.tensor_tensor(rstd[:], var[:], minus_half[:], ALU.pow).then_inc(S["rstd_made"], 1)

        @block.vector
        def _(dve):
            credit(dve, "tn_made", "pooled_made")
            dve.sem_inc(S["gated"], 2)
            for i in range(2):
                dve.sem_inc(w_stored[i], DMA)
            nc.vector.memset(zeros[:], 0.0)
            nc.vector.memset(minus_half[:], -0.5).then_inc(S["filled"], 1)
            STEPS = 4
            with dve.Fori(0, B) as b:
                wait_first(dve, S["filled"], at("pooled", b))

                def normalise(g, i, filling):
                    n = b * GROUPS + g

                    def step(x, k):
                        x.then_inc(S["step"], 1)
                        dve.wait_ge(S["step"], n * STEPS + k)
                    dve.wait_ge(t_loaded[i], (b * (GROUPS // 2) + filling + 1) * DMA)
                    for tt in range(TILES):
                        done = nc.vector.bn_stats(stats[i][:, tt, :], t_in[i][:, tt, :])
                    step(done, 1)
                    variance(dve, nc, stats[i], both, differ, spread, mean, var, C, EPS,
                             lambda x, k: step(x, 1 + k)).then_inc(S["stats_made"], 1)
                    wait(dve, "rstd_made", n + 1)
                    wait(dve, "turned", n - 1)
                    for tt in range(TILES):
                        done = nc.vector.tensor_scalar(tn_group[i][:, tt, :], t_in[i][:, tt, :], mean[:, tt:tt + 1],
                                                       rstd[:, tt:tt + 1], ALU.subtract, ALU.mult)
                    done.then_inc(S["tn_made"], 1)
                    wait(dve, "tn_made", n + 1)
                    nc.vector.tensor_copy(tn[:, bass.ds(g * TILES, TILES), :], tn_group[i][:]).then_inc(S["kept"], 1)
                groups(dve, normalise)
                wait_first(dve, S["filled"], at("logits_made", (b + 1) * GROUPS))
                nc.vector.max(top[:], logits[:]).then_inc(S["maxed"], 1)
                wait(dve, "maxed", b + 1)
                nc.vector.tensor_scalar(minus_top[:], top[:, 0:1], -1.0, None, ALU.mult).then_inc(S["topped"], 1)
                nc.vector.match_replace(left[:], top[:], logits[:], TAKEN).then_inc(S["replaced"], 1)
                wait(dve, "exped", b + 1)
                nc.vector.reciprocal(scale[:], total[:]).then_inc(S["scaled"], 1)
                wait_first(dve, S["filled"], at("replaced", b + 1), at("scaled", b + 1))

                def pool(g, i, filling):
                    n = b * GROUPS + g
                    cols = bass.ds(g * G, G)
                    dve.wait_ge(w_stored[i], (b * (GROUPS // 2) + filling + 1) * DMA)
                    wait(dve, "w_turned", n - 1)
                    nc.vector.scalar_tensor_tensor(weights[i][:], left[:, cols], TAKEN, probs[:, cols], ALU.is_le,
                                                   ALU.mult).then_inc(S["masked"], 1)
                    wait(dve, "masked", n + 1)
                    nc.vector.tensor_scalar(weights[i][:], weights[i][:], scale[:], None, ALU.mult).then_inc(S["weights_made"], 1)
                groups(dve, pool)
                wait(dve, "pool_turned", b + 1)
                nc.vector.tensor_copy(p.pooled[:, :, bass.ds(b, 1)].rearrange("c e o -> c (e o)"), pooled_ps[:]).then_inc(S["pooled_made"], 1)


def experts(p):
    nc, B, C, E = p.nc, p.B, p.C, p.E
    HID = p.ins["L1_ffn_weight1"].shape[2]
    SIDE = 32
    EG = P // SIDE
    GROUPS = E // EG
    KC = HID // P
    SLOTS = 2
    assert HID == BANK and KC * C == BANK
    w1 = p.ins["L1_ffn_weight1"]
    w2 = p.ins["L1_ffn_weight2"]
    with ExitStack() as ctx:
        sb = lambda n, s, dt=F32: ctx.enter_context(nc.sbuf_tensor(n, s, dt))
        ps = lambda n, s: ctx.enter_context(nc.psum_tensor(n, s, F32))
        w1_sb = [sb(f"w1_sb{i}", [C, EG, HID]) for i in range(SLOTS)]
        b1_sb = [sb(f"b1_sb{i}", [P, HID]) for i in range(SLOTS)]
        w2_sb = [sb(f"w2_sb{i}", [P, EG, KC, C]) for i in range(SLOTS)]
        pooled_g = [sb(f"pooled_g{i}", [C, EG, SIDE]) for i in range(2)]
        pre = [sb(f"pre{i}", [P, HID]) for i in range(2)]
        hid = [sb(f"hid{i}", [P, HID]) for i in range(2)]
        hid_turned = [sb(f"hid_turned{i}", [P, KC, P]) for i in range(2)]
        out_all = sb("out_all", [P, GROUPS, C])
        h_ps = [ps(f"h_ps{i}", [P, HID]) for i in range(2)]
        t_ps = [ps(f"t_ps{i}", [P, KC, P]) for i in range(2)]
        o_ps = [ps(f"e_o_ps{i}", [P, C]) for i in range(2)]
        w1_loaded = [p.sem(f"w1_loaded{i}") for i in range(SLOTS)]
        b1_loaded = [p.sem(f"b1_loaded{i}") for i in range(SLOTS)]
        w2_loaded = [p.sem(f"w2_loaded{i}") for i in range(SLOTS)]
        names = ("cleared gathered first added geluted turned taken second kept stored").split()
        S = {n: p.sem("ex_" + n) for n in names}
        CREDITS = {"first": 2, "second": 2, "added": 2, "taken": 2, "kept": 2, "geluted": 2, "turned": 2}
        block = ctx.enter_context(nc.Block())

        def at(name, count):
            return S[name], count + CREDITS.get(name, 0)

        def wait(engine, name, count):
            engine.wait_ge(*at(name, count))

        def credit(engine, *which):
            for name in which:
                engine.sem_inc(S[name], CREDITS[name])

        def groups(engine, run):
            with engine.Fori(0, GROUPS // 2) as g2:
                for i in range(2):
                    run(2 * g2 + i, i, g2)

        @block.sync
        def _(sp):
            sp.wait_ge(S["cleared"], 1)

            def load(g, i, filling):
                at = sp.snap(g * EG)
                wait(sp, "first", g - 1)
                sp.dma_start(w1_sb[i][:], w1[bass.ds(at, EG), 0:C, :].rearrange("e c h -> c e h")).then_inc(w1_loaded[i], DMA)
                at = sp.snap(g * EG)
                wait(sp, "second", g - 1)
                sp.dma_start(w2_sb[i][:], w2[bass.ds(at, EG), 0:HID, :].rearrange("e (p k) c -> p e k c", k=KC)).then_inc(w2_loaded[i], DMA)
            groups(sp, load)

        @block.tensor
        def _(pe):
            credit(pe, "first", "second", "turned")

            def run(g, i, filling):
                wait_first(pe, S["cleared"], at("gathered", g + 1), at("added", g - 1), (w1_loaded[i], (filling + 1) * DMA))
                for j in range(EG):
                    done = nc.tensor.matmul(h_ps[i][j * SIDE:(j + 1) * SIDE, :], pooled_g[i][:, j, :], w1_sb[i][:, j, :],
                                            start=True, stop=True)
                done.then_inc(S["first"], 1)
                wait(pe, "geluted", g + 1)
                wait(pe, "taken", g - 1)
                for k in range(KC):
                    done = nc.tensor.transpose(t_ps[i][:, k, :], hid[i][:].rearrange("p (q k) -> p k q", k=KC)[:, k, :], p.ident[:])
                done.then_inc(S["turned"], 1)
                wait_first(pe, S["cleared"], at("taken", g + 1), at("kept", g - 1), (w2_loaded[i], (filling + 1) * DMA))
                for j in range(EG):
                    for k in range(KC):
                        done = nc.tensor.matmul(o_ps[i][j * SIDE:(j + 1) * SIDE, :], hid_turned[i][:, k, j * SIDE:(j + 1) * SIDE],
                                                w2_sb[i][:, j, k, :], start=k == 0, stop=k == KC - 1)
                done.then_inc(S["second"], 1)
            groups(pe, run)

        @block.vector
        def _(dve):
            credit(dve, "added", "kept")
            for i in range(2):
                nc.vector.memset(pooled_g[i][:], 0.0)
                done = nc.vector.memset(b1_sb[i][:], 0.0)
            done.then_inc(S["cleared"], 1)
            dve.wait_ge(S["cleared"], 1)

            def run(g, i, filling):
                wait(dve, "first", g - 1)
                nc.vector.tensor_copy(pooled_g[i][:, :, 0:B], p.pooled[:, bass.ds(g * EG, EG), :]).then_inc(S["gathered"], 1)
                wait(dve, "first", g + 1)
                wait(dve, "geluted", g - 1)
                dve.wait_ge(b1_loaded[i], (filling + 1) * EG * DMA)
                nc.vector.tensor_tensor(pre[i][:], h_ps[i][:], b1_sb[i][:], ALU.add).then_inc(S["added"], 1)
                wait(dve, "second", g + 1)
                nc.vector.tensor_copy(out_all[:, bass.ds(g, 1), :].rearrange("p o c -> p (o c)"), o_ps[i][:]).then_inc(S["kept"], 1)
            groups(dve, run)

        @block.scalar
        def _(act):
            credit(act, "taken", "geluted")
            act.wait_ge(S["cleared"], 1)

            def run(g, i, filling):
                for j in range(EG):
                    wait(act, "added", g - 1)
                    act.dma_start(b1_sb[i][j * SIDE:j * SIDE + B, :],
                                  w1[bass.ds(g * EG + j, 1), C, :].rearrange("o h -> (o h)").partition_broadcast(B)).then_inc(b1_loaded[i], DMA)
                wait(act, "added", g + 1)
                wait(act, "turned", g - 1)
                nc.scalar.activation(hid[i][:], pre[i][:], ACT.Gelu).then_inc(S["geluted"], 1)
                wait(act, "turned", g + 1)
                wait(act, "second", g - 1)
                nc.scalar.copy(hid_turned[i][:], t_ps[i][:]).then_inc(S["taken"], 1)
            groups(act, run)
            wait(act, "kept", GROUPS)
            for j in range(EG):
                act.dma_start(p.expert_d.rearrange("(g j) b c -> j b g c", j=EG)[j],
                              out_all[j * SIDE:j * SIDE + B, :, :]).then_inc(S["stored"], DMA)
            act.wait_ge(S["stored"], EG * DMA)


def combine(p):
    nc, B, N, C, E = p.nc, p.B, p.N, p.C, p.E
    HID = p.ins["L1_ffn_weight1"].shape[2]
    TILES = 4
    G = TILES * P
    GROUPS = N // G
    out_v = p.out.rearrange("b h w c -> (b h w) c")
    with ExitStack() as ctx:
        sb = lambda n, s, dt=F32: ctx.enter_context(nc.sbuf_tensor(n, s, dt))
        outs, b2 = sb("outs", [E, B, C]), sb("b2", [E, C])
        weights = [sb(f"f_weights{i}", [E, G]) for i in range(2)]
        tokens = [sb(f"f_tokens{i}", [P, TILES, C]) for i in range(2)]
        result = [sb(f"result{i}", [P, TILES, C]) for i in range(2)]
        acc = [ctx.enter_context(nc.psum_tensor(f"acc{i}", [P, TILES, C], F32)) for i in range(2)]
        ready, made, added = p.sem("fi_ready"), p.sem("fi_made"), p.sem("fi_added")
        outs_loaded = p.sem("outs_loaded")
        loaded = [p.sem(f"fi_loaded{i}") for i in range(2)]
        stored = [p.sem(f"fi_stored{i}") for i in range(2)]
        block = ctx.enter_context(nc.Block())

        @block.sync
        def _(sp):
            sp.dma_start(outs[:], p.expert_d).then_inc(outs_loaded, DMA)
            sp.dma_start(b2[:], p.ins["L1_ffn_weight2"][:, HID, :]).then_inc(outs_loaded, DMA)
            with sp.Fori(0, B * GROUPS // 2) as n2:
                for i in range(2):
                    n = 2 * n2 + i
                    at = sp.snap(n * G)
                    sp.wait_ge(added, n + 1)
                    sp.dma_start(weights[i][:], p.chosen_d[:, bass.ds(at, G)]).then_inc(loaded[i], DMA)
                    sp.dma_start(tokens[i][:], p.t2_d[bass.ds(at, G), :].rearrange("(t p) c -> p t c", p=P)).then_inc(loaded[i], DMA)

        @block.tensor
        def _(pe):
            pe.sem_inc(made, 2)
            pe.wait_ge(ready, 1)
            with pe.Fori(0, B) as b:
                with pe.Fori(0, GROUPS // 2) as g2:
                    for i in range(2):
                        n = b * GROUPS + 2 * g2 + i
                        wait_first(pe, ready, (added, n + 1), (loaded[i], (b * (GROUPS // 2) + g2 + 1) * 2 * DMA))
                        for tt in range(TILES):
                            done = nc.tensor.matmul(acc[i][:, tt, :], weights[i][:, tt * P:(tt + 1) * P], outs[:, bass.ds(b, 1), :],
                                                    start=True, stop=True)
                        done.then_inc(made, 1)

        @block.vector
        def _(dve):
            dve.sem_inc(added, 2)
            for i in range(2):
                dve.sem_inc(stored[i], DMA)
            dve.wait_ge(outs_loaded, 2 * DMA)
            nc.vector.tensor_tensor(outs[:], outs[:], b2[:].unsqueeze(1).to_broadcast([E, B, C]), ALU.add).then_inc(ready, 1)
            with dve.Fori(0, B * GROUPS // 2) as n2:
                for i in range(2):
                    n = 2 * n2 + i
                    dve.wait_ge(made, n + 1 + 2)
                    dve.wait_ge(stored[i], (n2 + 1) * DMA)
                    nc.vector.tensor_tensor(result[i][:], acc[i][:], tokens[i][:], ALU.add).then_inc(added, 1)

        @block.scalar
        def _(act):
            with act.Fori(0, B * GROUPS // 2) as n2:
                for i in range(2):
                    n = 2 * n2 + i
                    act.wait_ge(added, n + 1 + 2)
                    act.dma_start(out_v[bass.ds(n * G, G), :].rearrange("(t p) c -> p t c", p=P), result[i][:]).then_inc(stored[i], DMA)
            for i in range(2):
                act.wait_ge(stored[i], (B * GROUPS // 2 + 1) * DMA)


INPUTS = ["x", "L0_conv_Wq", "L0_conv_Wk", "L0_conv_Wv", "L0_conv_gamma", "L1_attn_W_kv", "L1_attn_q_proj",
          "L1_ffn_gate_w", "L1_ffn_gate_b", "L1_ffn_weight1", "L1_ffn_weight2"]


def program(nc, ins, out):
    with ExitStack() as whole:
        p = Program(nc, whole, ins, out)
        prepare(p)
        project(p)
        pairs(p)
        prefix(p)
        choose(p)
        experts(p)
        combine(p)


def kernel(**inputs):
    import numpy as np
    import concourse.bacc as bacc
    from concourse.bass_utils import run_bass_kernel_spmd

    nc = bacc.Bacc("TRN2", target_bir_lowering=False, num_devices=1)
    arrays, ins = {}, {}
    for name in INPUTS:
        a = np.ascontiguousarray(inputs[name])
        a = a.reshape(a.shape or (1,))
        arrays[f"in_{name}"] = a
        ins[name] = nc.dram_tensor(f"in_{name}", a.shape, mybir.dt.from_np(a.dtype), kind="ExternalInput").ap()
    out = nc.dram_tensor("out_0", inputs["x"].shape, F32, kind="ExternalOutput").ap()
    program(nc, ins, out)
    r = run_bass_kernel_spmd(nc, [arrays], core_ids=[0])
    return r.results[0]["out_0"]
```

```python
import concourse.bass as bass
from concourse import mybir
from contextlib import ExitStack

ALU = mybir.AluOpType
ACT = mybir.ActivationFunctionType
AX = mybir.AxisListType
F32 = mybir.dt.float32
F32R = mybir.dt.float32r

P = 128
BANK = 512
PARTS = 4
DMA = 16


def plain(ap):
    return ap.bitcast(F32)


class Program:

    def __init__(self, nc, whole, ins, out):
        self.nc, self.whole, self.ins, self.out = nc, whole, ins, out
        self.B, self.H, self.W, self.C = ins["x"].shape
        self.N = self.H * self.W
        self.D = ins["L0_conv_Wq"].shape[1]
        self.NT = self.N // P
        self.KR = PARTS * self.D + 2
        scratch = lambda name, shape, dt: nc.dram_tensor(name, shape, dt).ap()
        self.f_d = scratch("f_scratch", (self.KR, self.B * self.N), F32)
        self.g_d = scratch("g_scratch", (PARTS * self.D, self.B * self.N), F32)
        self.hv_d = scratch("hv_scratch", (P, self.B * self.N), F32)
        self.y_d = scratch("y_scratch", (self.B * self.N * self.C + self.N,), F32)
        self.y_tok = self.y_d[0:self.B * self.N * self.C].rearrange("(t c) -> t c", c=self.C)
        self.t2_d = scratch("t2_scratch", (self.B * self.N, self.C), F32)
        self.HEADS = ins["L1_attn_q_proj"].shape[0]
        self.E = ins["L1_ffn_gate_w"].shape[0]
        self.EG = 4
        self.expert_d = scratch("expert_scratch", (self.E, self.B, self.C), F32)

    def sem(self, name):
        return self.whole.enter_context(self.nc.semaphore(name))

    def const(self, name, shape, dt=F32):
        return self.whole.enter_context(self.nc.sbuf_tensor(name, shape, dt))


def wait_first(engine, passed, *waits):
    waits = [(sem, engine.to_reg(value)) for sem, value in waits]
    engine.wait_ge(passed, 1)
    for sem, value in waits:
        engine.wait_ge(sem, value)


def prepare(p):
    nc, C, D = p.nc, p.C, p.D
    p.ident = p.const("ident", [P, P])
    p.ones = p.const("ones", [P, P])
    p.wf = p.const("wf", [C, PARTS * D])
    p.wg = p.const("wg", [C, PARTS * D])
    p.wv = p.const("wv", [C, C])
    p.low_f = p.const("low_f", [PARTS * D, 1])
    p.low_g = p.const("low_g", [PARTS * D, 1])
    p.low_2 = p.const("low_2", [2, 1])
    p.gamma = p.const("gamma", [P, 1])
    with ExitStack() as ctx:
        sb = lambda n, s, dt=F32: ctx.enter_context(nc.sbuf_tensor(n, s, dt))
        wq = sb("wq", [C, D])
        wk = sb("wk", [C, D])
        steps = sb("steps", [PARTS * D, 3])
        loaded = p.sem("prep_loaded")
        filled = p.sem("prep_filled")
        chosen = p.sem("prep_chosen")
        stepped = p.sem("prep_stepped")
        block = ctx.enter_context(nc.Block())

        @block.sync
        def _(sp):
            sp.dma_start(wq[:], p.ins["L0_conv_Wq"]).then_inc(loaded, DMA)
            sp.dma_start(wk[:], p.ins["L0_conv_Wk"]).then_inc(loaded, DMA)
            sp.dma_start(p.wv[:], p.ins["L0_conv_Wv"]).then_inc(loaded, DMA)
            sp.dma_start(p.gamma[:], p.ins["L0_conv_gamma"].partition_broadcast(P)).then_inc(loaded, DMA)
            sp.wait_ge(loaded, 4 * DMA)

        @block.gpsimd
        def _(pool):
            nc.gpsimd.memset(p.ident[:], 0.0).then_inc(filled, 1)
            nc.gpsimd.memset(p.ones[:], 1.0).then_inc(filled, 1)
            nc.gpsimd.memset(steps[:], 1.0).then_inc(filled, 1)
            nc.gpsimd.memset(p.low_2[:], 1.0).then_inc(filled, 1)
            pool.wait_ge(filled, 4)
            nc.gpsimd.affine_select(out=p.ident[:], in_=p.ident[:], compare_op=ALU.not_equal, fill=1.0, base=0,
                                    pattern=[[-1, P]], channel_multiplier=1).then_inc(chosen, 1)
            nc.gpsimd.affine_select(out=steps[:], in_=steps[:], compare_op=ALU.is_ge, fill=0.0, base=-D,
                                    pattern=[[-D, 3]], channel_multiplier=1).then_inc(chosen, 1)
            nc.gpsimd.affine_select(out=p.low_2[:], in_=p.low_2[:], compare_op=ALU.is_ge, fill=0.0, base=-1,
                                    pattern=[[0, 1]], channel_multiplier=1).then_inc(chosen, 1)

        @block.vector
        def _(dve):
            dve.wait_ge(chosen, 3)
            nc.vector.tensor_copy(p.low_f[:], steps[:, 1:2])
            nc.vector.tensor_tensor(p.low_g[:], steps[:, 0:1], steps[:, 1:2], ALU.subtract).then_inc(stepped, 1)
            dve.wait_ge(stepped, 1)
            nc.vector.tensor_tensor(p.low_g[:], p.low_g[:], steps[:, 2:3], ALU.add)

        @block.scalar
        def _(act):
            act.wait_ge(loaded, 4 * DMA)
            for part in range(PARTS):
                cols = slice(part * D, (part + 1) * D)
                nc.scalar.mul(p.wf[:, cols], wq[:], -1.0 if part < 2 else 1.0)
                nc.scalar.mul(p.wg[:, cols], wk[:], -1.0 if part % 2 == 0 else 1.0)


def project(p):
    nc, B, N, R, KR = p.nc, p.B, p.N, PARTS * p.D, p.KR
    TILES = BANK // P
    CHUNKS = p.NT // TILES
    x_v = p.ins["x"].rearrange("b h w c -> b (h w c)").rearrange("b (p n) -> b p n", p=P)
    with ExitStack() as ctx:
        sb = lambda n, s, dt=F32: ctx.enter_context(nc.sbuf_tensor(n, s, dt))
        ps = lambda n, s: ctx.enter_context(nc.psum_tensor(n, s, F32))
        xin = [sb(f"xin{i}", [P, BANK]) for i in range(2)]
        xt = [sb(f"xt{i}", [P, BANK]) for i in range(2)]
        f_high = [sb(f"f_high{i}", [R, BANK], F32R) for i in range(2)]
        g_high = [sb(f"g_high{i}", [R, BANK], F32R) for i in range(2)]
        f_rows = [sb(f"f_rows{i}", [KR, BANK], F32R) for i in range(2)]
        hv = [sb(f"hv{i}", [P, BANK]) for i in range(2)]
        g_rows = sb("g_rows", [R, B * N], F32R)
        xt_ps = [ps(f"xt_ps{i}", [P, BANK]) for i in range(2)]
        f_ps = [ps(f"f_ps{i}", [P, BANK]) for i in range(2)]
        g_ps = [ps(f"g_ps{i}", [P, BANK]) for i in range(2)]
        hv_ps = [ps(f"hv_ps{i}", [P, BANK]) for i in range(2)]
        x_loaded = [p.sem(f"x_loaded{i}") for i in range(2)]
        x_turned = p.sem("x_turned")
        xt_ready = p.sem("xt_ready")
        f_made, g_made, hv_made = p.sem("f_made"), p.sem("g_made"), p.sem("hv_made")
        f_rounded, g_rounded = p.sem("f_rounded"), p.sem("g_rounded")
        f_split, g_split = p.sem("f_split"), p.sem("g_split")
        hv_ready = p.sem("hv_ready")
        f_stored = [p.sem(f"f_stored{i}") for i in range(2)]
        hv_stored = [p.sem(f"hv_stored{i}") for i in range(2)]
        g_stored = p.sem("g_stored")
        filled = p.sem("rows_filled")
        PAIRS = B * CHUNKS // 2
        block = ctx.enter_context(nc.Block())

        def done(n):
            return n + 3

        def chunks(engine, run):
            with engine.Fori(0, PAIRS - 1) as n2:
                run(2 * n2, 0, n2)
                run(2 * n2 + 1, 1, n2)
            run(2 * PAIRS - 2, 0, PAIRS - 1)
            run(2 * PAIRS - 1, 1, PAIRS - 1)

        def has_next(n):
            return not isinstance(n, int) or n < 2 * PAIRS - 1

        @block.sync
        def _(sp):
            def load(b):
                with sp.Fori(0, CHUNKS // 2) as c2:
                    for i in range(2):
                        sp.wait_ge(x_turned, b * CHUNKS + 2 * c2 + i + 1)
                        sp.dma_start(xin[i][:], x_v[b, :, bass.ds((2 * c2 + i) * BANK, BANK)]).then_inc(x_loaded[i], DMA)

            def store_g(b):
                at = sp.snap(b * N)
                sp.wait_ge(g_split, done((b + 1) * CHUNKS - 1))
                sp.dma_start(p.g_d[:, bass.ds(at, N)], plain(g_rows[:, bass.ds(at, N)])).then_inc(g_stored, DMA)
            load(0)
            with sp.Fori(1, B) as b:
                load(b)
                store_g(b - 1)
            store_g(B - 1)
            sp.wait_ge(g_stored, B * DMA)

        @block.tensor
        def _(pe):
            for sem in (x_turned, hv_made):
                pe.sem_inc(sem, 2)

            def turn(n, i, half):
                pe.wait_ge(x_loaded[i], DMA * (half + 1))
                pe.wait_ge(xt_ready, n + 1)
                for t in range(TILES):
                    last = nc.tensor.transpose(xt_ps[i][:, t * P:(t + 1) * P], xin[i][:, t * P:(t + 1) * P], p.ident[:])
                last.then_inc(x_turned, 1)

            def run(n, i, half):
                if has_next(n):
                    turn(n + 1, 1 - i, half + i)
                pe.wait_ge(xt_ready, done(n))
                pe.wait_ge(f_split, n + 1)
                nc.tensor.matmul(f_ps[i][0:R, :], p.wf[:], xt[i][:], start=True, stop=True).then_inc(f_made, 1)
                pe.wait_ge(g_split, n + 1)
                nc.tensor.matmul(g_ps[i][0:R, :], p.wg[:], xt[i][:], start=True, stop=True).then_inc(g_made, 1)
                pe.wait_ge(hv_ready, n + 1)
                for t in range(TILES):
                    last = nc.tensor.matmul(hv_ps[i][:, t * P:(t + 1) * P], xt[i][:, t * P:(t + 1) * P], p.wv[:],
                                            start=True, stop=True)
                last.then_inc(hv_made, 1)
            turn(0, 0, 0)
            chunks(pe, run)

        @block.vector
        def _(dve):
            for sem in (f_split, g_split):
                dve.sem_inc(sem, 2)
            for i in range(2):
                dve.sem_inc(f_stored[i], DMA)
                nc.vector.memset(plain(f_rows[i][R:KR, :]), 1.0).then_inc(filled, 1)

            def run(n, i, half):
                dve.wait_ge(f_made, n + 1)
                nc.vector.tensor_copy(f_high[i][:], f_ps[i][0:R, :]).then_inc(f_rounded, 1)
                dve.wait_ge(g_made, n + 1)
                nc.vector.tensor_copy(g_high[i][:], g_ps[i][0:R, :]).then_inc(g_rounded, 1)
                dve.wait_ge(f_rounded, n + 1)
                dve.wait_ge(f_stored[i], DMA * (half + 1))
                nc.vector.scalar_tensor_tensor(f_rows[i][0:R, :], f_ps[i][0:R, :], p.low_f[:], plain(f_high[i][:]),
                                               ALU.mult, ALU.subtract).then_inc(f_split, 1)
                dve.wait_ge(g_rounded, n + 1)
                b, c = n // CHUNKS, n % CHUNKS
                rows = g_rows[0:R, bass.ds(b * N, N)].rearrange("r (q t) -> r t q", t=p.NT)
                rows = rows[:, bass.ds(c * TILES, TILES), :]
                nc.vector.scalar_tensor_tensor(
                    rows, g_ps[i][0:R, :].rearrange("r (t q) -> r t q", q=P), p.low_g[:],
                    plain(g_high[i][:]).rearrange("r (t q) -> r t q", q=P), ALU.mult, ALU.subtract).then_inc(g_split, 1)
            chunks(dve, run)

        @block.scalar
        def _(act):
            for sem in (xt_ready, hv_ready):
                act.sem_inc(sem, 2)
            for i in range(2):
                act.sem_inc(hv_stored[i], DMA)
            act.wait_ge(filled, 2)

            def take(n, i):
                act.wait_ge(x_turned, done(n))
                act.wait_ge(hv_made, n + 1)
                nc.scalar.copy(xt[i][:], xt_ps[i][:]).then_inc(xt_ready, 1)

            def run(n, i, half):
                if has_next(n):
                    take(n + 1, 1 - i)
                act.wait_ge(hv_made, done(n))
                act.wait_ge(hv_stored[i], DMA * (half + 1))
                nc.scalar.copy(hv[i][:], hv_ps[i][:]).then_inc(hv_ready, 1)
                act.wait_ge(f_split, done(n))
                act.dma_start(p.f_d[:, bass.ds(n * BANK, BANK)], plain(f_rows[i][:])).then_inc(f_stored[i], DMA)
                act.wait_ge(hv_ready, done(n))
                act.dma_start(p.hv_d[:, bass.ds(n * BANK, BANK)], hv[i][:]).then_inc(hv_stored[i], DMA)
            take(0, 0)
            chunks(act, run)
            for i in range(2):
                act.wait_ge(f_stored[i], DMA * (PAIRS + 1))
                act.wait_ge(hv_stored[i], DMA * (PAIRS + 1))


def pairs(p):
    nc, B, N, R, KR = p.nc, p.B, p.N, PARTS * p.D, p.KR
    M = 2 * BANK
    BLOCKS = B * N // M
    PER_IMAGE = N // M
    GROUP = 4
    GROUPS = p.NT // GROUP
    HALVES = M // BANK
    assert GROUPS * P == M and BLOCKS % 2 == 0 and GROUPS % 2 == 0
    USES = GROUPS * (2 * GROUP + 1) + HALVES
    FIRST_USES = GROUPS * (2 * GROUP + 1)
    x_v = p.ins["x"].rearrange("b h w c -> b (h w c)").rearrange("b (p n) -> b p n", p=P)
    with ExitStack() as ctx:
        sb = lambda n, s, dt=F32: ctx.enter_context(nc.sbuf_tensor(n, s, dt))
        ps = lambda n, s: ctx.enter_context(nc.psum_tensor(n, s, F32))
        f_all = [sb(f"f_all{i}", [KR, N], F32R) for i in range(2)]
        g_cols = [sb(f"g_cols{i}", [KR, M], F32R) for i in range(2)]
        f_tiles = [sb(f"f_tiles{i}", [KR, GROUP * P], F32R) for i in range(2)]
        hv_tiles = [sb(f"hv_tiles{i}", [P, GROUP * P]) for i in range(2)]
        g_tile = [sb(f"g_tile{i}", [KR, P], F32R) for i in range(2)]
        probs = [sb(f"probs{i}", [P, M]) for i in range(GROUP)]
        sums = [sb(f"sums{i}", [P, M]) for i in range(2)]
        x_res = [sb(f"x_res{i}", [P, M]) for i in range(2)]
        att_sb = [sb(f"att_sb{i}", [P, M]) for i in range(2)]
        y_out = [sb(f"y_out{i}", [P, M]) for i in range(2)]
        total, inv = sb("sums_total", [P, M]), sb("inv", [P, P])
        part_max = [sb(f"part_max{i}", [P, 2 * GROUP]) for i in range(2)]
        pm_max = sb("pm_max", [P, 2])
        row = sb("row", [2, P])
        row_high = sb("row_high", [2, P], F32R)
        scores = [ps(f"scores{i}", [P, M]) for i in range(2)]
        att = ps("att", [P, M])
        side = [ps(f"side{i}", [P, BANK]) for i in range(2)]

        tiles_loaded = [p.sem(f"tiles_loaded{i}") for i in range(2)]
        g_tile_loaded = [p.sem(f"g_tile_loaded{i}") for i in range(2)]
        g_tile_cleared = p.sem("g_tile_cleared")
        f_loaded = [p.sem(f"f_loaded{i}") for i in range(2)]
        g_loaded = [p.sem(f"g_loaded{i}") for i in range(2)]
        x_res_loaded = [p.sem(f"x_res_loaded{i}") for i in range(2)]
        scored, exped = p.sem("scored"), p.sem("exped")
        weighed, summed = p.sem("weighed"), p.sem("summed")
        side_full, side_free = p.sem("side_full"), p.sem("side_free")
        max_ready, shift_ready = p.sem("max_ready"), p.sem("shift_ready")
        row_step = p.sem("row_step")
        att_copied = p.sem("att_copied")
        norm_step = p.sem("norm_step")
        y_ready = p.sem("y_ready")
        y_stored = [p.sem(f"y_stored{i}") for i in range(2)]
        block = ctx.enter_context(nc.Block())

        def image(k):
            return k // PER_IMAGE

        def first_column(k):
            return (k % PER_IMAGE) * M

        def each_block(engine, run):
            with engine.Fori(0, BLOCKS // 2 - 1) as pair:
                run(2 * pair, 0, pair)
                run(2 * pair + 1, 1, pair)
            run(BLOCKS - 2, 0, BLOCKS // 2 - 1)
            run(BLOCKS - 1, 1, BLOCKS // 2 - 1)

        def is_from(k, block):
            return isinstance(k, int) and k >= block

        def each_group(engine, run):
            run(0, 0, 0)
            with engine.Fori(0, GROUPS // 2 - 1) as g2:
                run(2 * g2 + 1, 1, g2)
                run(2 * g2 + 2, 0, g2 + 1)
            run(GROUPS - 1, 1, GROUPS // 2 - 1)

        def is_group(gi, which):
            return isinstance(gi, int) and gi == which

        def first_use(k):
            return k * USES + FIRST_USES

        TILE_USES = 2 * GROUP + 1
        AHEAD = 2

        def chunk_use(gi, slot, c):
            if is_group(gi, 0):
                return c, c % 2
            late = 0 if c < AHEAD else 1
            return gi * TILE_USES - 1 + c + late, (slot + 1 + c + late) % 2

        def shift_use(gi, slot):
            return gi * TILE_USES - 1 + AHEAD, (slot + 1 + AHEAD) % 2

        LAST_SHIFT = GROUPS * TILE_USES - 1
        FILLS = GROUPS // 2

        @block.sync
        def _(sp):
            def load_f(first, i):
                sp.dma_start(plain(f_all[i][:]), p.f_d[:, bass.ds(first, N)]).then_inc(f_loaded[i], DMA)

            def load_g(first, i):
                sp.dma_start(plain(g_cols[i][0:R, :]), p.g_d[:, bass.ds(first, M)]).then_inc(g_loaded[i], DMA)

            def load_g_tile(first, slot):
                sp.dma_start(plain(g_tile[slot][0:R, :]), p.g_d[:, bass.ds(first, P)]).then_inc(g_tile_loaded[slot], DMA)

            load_f(0, 0)
            for slot in range(2):
                load_g_tile(slot * P, slot)
            load_g(0, 0)
            load_f(image(1) * N, 1)
            with sp.Fori(1, GROUPS // 2) as g2:
                for slot in range(2):
                    first = sp.snap((2 * g2 + slot) * P)
                    sp.wait_ge(max_ready, 2 * g2 + slot + 1)
                    load_g_tile(first, slot)

            def run(k, i, pair):
                def group(gi, slot, filling):
                    g = k * GROUPS + gi
                    tiles_at = sp.snap(image(k) * N + gi * (GROUP * P))
                    tile_at = sp.snap((k + 1) * M + gi * P)
                    g_at = sp.snap((k + 1) * M)
                    f_at = sp.snap(image(k + 2) * N)
                    sp.wait_ge(weighed, g * GROUP + GROUP)
                    sp.dma_start(plain(f_tiles[slot][:]), p.f_d[:, bass.ds(tiles_at, GROUP * P)]).then_inc(tiles_loaded[slot], DMA)
                    sp.dma_start(hv_tiles[slot][:], p.hv_d[:, bass.ds(tiles_at, GROUP * P)]).then_inc(tiles_loaded[slot], DMA)
                    if not is_from(k, BLOCKS - 1):
                        sp.wait_ge(max_ready, g + GROUPS + 1)
                        load_g_tile(tile_at, slot)
                    if is_group(gi, 0) and not is_from(k, BLOCKS - 1):
                        sp.wait_ge(weighed, k * p.NT + 2 * GROUP)
                        load_g(g_at, 1 - i)
                        if not is_from(k, BLOCKS - 2):
                            sp.wait_ge(max_ready, (k + 1) * GROUPS + 2)
                            load_f(f_at, i)
                    if is_group(gi, 0) and not (isinstance(k, int) and k < 2):
                        store_y(k - 2, i)
                each_group(sp, group)

            def store_y(k, i):
                at = sp.snap(image(k) * (P * N) + first_column(k))
                target = p.y_d[bass.ds(at, P * N)].rearrange("(p n) -> p n", p=P)[:, 0:M]
                sp.wait_ge(y_ready, k + 3)
                sp.dma_start(target, y_out[i][:]).then_inc(y_stored[i], DMA)

            run(0, 0, 0)
            run(1, 1, 0)
            with sp.Fori(1, BLOCKS // 2 - 1) as pair:
                run(2 * pair, 0, pair)
                run(2 * pair + 1, 1, pair)
            run(BLOCKS - 2, 0, BLOCKS // 2 - 1)
            run(BLOCKS - 1, 1, BLOCKS // 2 - 1)
            store_y(BLOCKS - 2, 0)
            store_y(BLOCKS - 1, 1)
            for i in range(2):
                sp.wait_ge(y_stored[i], DMA * (BLOCKS // 2 + 1))

        @block.tensor
        def _(pe):
            pe.sem_inc(weighed, 2 * GROUP)

            def chunk(use, bank, slot, side_i, c):
                pe.wait_ge(side_free, use + 1)
                nc.tensor.matmul(side[bank][:], g_tile[slot][:], f_all[side_i][:, c * BANK:(c + 1) * BANK],
                                 start=True, stop=True).then_inc(side_full, 1)

            def shift_rows(use, bank, tile):
                pe.wait_ge(side_free, use + 1)
                pe.wait_ge(max_ready, tile + 3)
                nc.tensor.matmul(side[bank][0:2, 0:P], pm_max[:], p.ident[:], start=True, stop=True).then_inc(side_full, 1)

            pe.wait_ge(g_tile_cleared, 1)
            pe.wait_ge(f_loaded[0], DMA)
            with pe.Fori(0, GROUPS // 2) as g2:
                for slot in range(2):
                    tile = 2 * g2 + slot
                    pe.wait_ge(g_tile_loaded[slot], DMA * (g2 + 1))
                    for c in range(2 * GROUP):
                        chunk(tile * TILE_USES + c, (slot + c) % 2, slot, 0, c)
                    shift_rows(tile * TILE_USES + 2 * GROUP, slot, tile)

            def run(k, i, pair):
                last = is_from(k, BLOCKS - 1)
                use = first_use(k)
                pe.wait_ge(shift_ready, (k + 1) * GROUPS)
                pe.wait_ge(g_loaded[i], DMA * (pair + 1))

                def weigh(t, s, slot, first=False, final=False, between=None):
                    pe.wait_ge(exped, t + 1)
                    if first:
                        pe.wait_ge(att_copied, k + 1)
                    for h in range(HALVES):
                        if h == 1 and between:
                            between()
                        cols = slice(h * BANK, (h + 1) * BANK)
                        done = nc.tensor.matmul(att[:, cols], hv_tiles[slot][:, s * P:(s + 1) * P], probs[s][:, cols],
                                                start=first, stop=final)
                    done.then_inc(weighed, 1)

                def group(gi, slot, filling):
                    g = k * GROUPS + gi
                    pe.wait_ge(tiles_loaded[slot], 2 * DMA * (k * FILLS + filling + 1))
                    if not last:
                        pe.wait_ge(g_tile_loaded[slot], DMA * ((k + 1) * FILLS + filling + 1))
                        if is_group(gi, 0):
                            pe.wait_ge(f_loaded[1 - i], DMA * (pair + 1 + i))
                    for s in range(GROUP):
                        t = g * GROUP + s
                        for h in range(HALVES):
                            cols = slice(h * BANK, (h + 1) * BANK)
                            done = nc.tensor.matmul(scores[s % 2][:, cols], f_tiles[slot][:, s * P:(s + 1) * P],
                                                    g_cols[i][:, cols], start=True, stop=True)
                        done.then_inc(scored, 1)
                        rows = None
                        if 2 * s == AHEAD and not is_group(gi, 0) and not last:
                            at, bank = shift_use(gi, slot)
                            rows = lambda: shift_rows(use + at, bank, g + GROUPS - 1)
                        if s > 0:
                            weigh(t - 1, s - 1, slot, first=is_group(gi, 0) and s == 1, between=rows)
                        elif not is_group(gi, 0):
                            weigh(t - 1, GROUP - 1, 1 - slot)
                        if not last:
                            for c in (2 * s, 2 * s + 1):
                                at, bank = chunk_use(gi, slot, c)
                                chunk(use + at, bank, slot, 1 - i, c)

                each_group(pe, group)
                weigh((k + 1) * p.NT - 1, GROUP - 1, 1, final=True)
                if not last:
                    shift_rows(use + LAST_SHIFT, LAST_SHIFT % 2, (k + 2) * GROUPS - 1)
                    use = use + GROUPS * TILE_USES
                pe.wait_ge(summed, (k + 1) * p.NT + GROUP)
                for h in range(HALVES):
                    pe.wait_ge(side_free, use + h + 1)
                    nc.tensor.matmul(side[h][:], p.ones[:], sums[i][:, h * BANK:(h + 1) * BANK],
                                     start=True, stop=True).then_inc(side_full, 1)
            each_block(pe, run)

        @block.scalar
        def _(act):
            def run(k, i, pair):
                def group(gi, slot, filling):
                    for s in range(GROUP):
                        t = (k * GROUPS + gi) * GROUP + s
                        act.wait_ge(scored, t + 1)
                        act.wait_ge(weighed, t + 1 + GROUP)
                        act.wait_ge(summed, t + 1)
                        nc.scalar.activation(probs[s][:], scores[s % 2][:], ACT.Exp).then_inc(exped, 1)
                each_group(act, group)
                act.wait_ge(y_ready, k + 1)
                act.dma_start(x_res[i][:], x_v[image(k), :, bass.ds(first_column(k), M)]).then_inc(x_res_loaded[i], DMA)
                act.wait_ge(weighed, (k + 1) * p.NT + 2 * GROUP)
                nc.scalar.copy(att_sb[i][:], att[:]).then_inc(att_copied, 1)
            each_block(act, run)

        @block.gpsimd
        def _(pool):
            pool.sem_inc(summed, GROUP)

            def run(k, i, pair):
                def group(gi, slot, filling):
                    for s in range(GROUP):
                        t = (k * GROUPS + gi) * GROUP + s
                        pool.wait_ge(exped, t + 1)
                        if is_group(gi, 0) and s == 0:
                            continue
                        if is_group(gi, 0) and s == 1:
                            nc.gpsimd.tensor_tensor(sums[i][:], probs[0][:], probs[1][:], ALU.add).then_inc(summed, 2)
                        else:
                            pool.wait_ge(summed, t + GROUP)
                            nc.gpsimd.tensor_tensor(sums[i][:], sums[i][:], probs[s][:], ALU.add).then_inc(summed, 1)
                each_group(pool, group)
            each_block(pool, run)

        @block.vector
        def _(dve):
            for slot in range(2):
                done = nc.vector.memset(plain(g_tile[slot][R:KR, :]), 0.0)
            done.then_inc(g_tile_cleared, 1)
            dve.sem_inc(max_ready, 2)
            dve.sem_inc(side_free, 2)
            dve.sem_inc(y_ready, 2)
            dve.sem_inc(att_copied, 1)
            for i in range(2):
                dve.sem_inc(y_stored[i], DMA)

            def chunk_max(use, bank, slot, c):
                dve.wait_ge(side_full, use + 1)
                nc.vector.reduce_max(part_max[slot][:, c:c + 1], side[bank][:], AX.X).then_inc(side_free, 1)

            def tile_max(use, slot):
                dve.wait_ge(side_free, use + 3)
                nc.vector.tensor_reduce(pm_max[:, 0:1], part_max[slot][:], AX.X, ALU.max)
                nc.vector.tensor_reduce(pm_max[:, 1:2], part_max[slot][:], AX.X, ALU.max, negate=True).then_inc(max_ready, 1)

            def shift(use, bank, tile, i, gi):
                dve.wait_ge(side_full, use + 1)
                nc.vector.tensor_copy(row[:], side[bank][0:2, 0:P]).then_inc(side_free, 1)
                dve.wait_ge(side_free, use + 3)
                nc.vector.tensor_copy(row_high[:], row[:]).then_inc(row_step, 1)
                dve.wait_ge(row_step, tile + 1)
                nc.vector.scalar_tensor_tensor(g_cols[i][R:KR, bass.ds(gi * P, P)], row[:], p.low_2[:],
                                               plain(row_high[:]), ALU.mult, ALU.subtract).then_inc(shift_ready, 1)

            def finish(k, i, half, gi):
                cols = bass.ds(gi * P, P)
                if is_group(gi, 0):
                    dve.wait_ge(att_copied, k + 2)
                    dve.wait_ge(y_stored[i], DMA * (half + 1))
                    dve.wait_ge(x_res_loaded[i], DMA * (half + 1))
                nc.vector.reciprocal(inv[:], total[:, cols]).then_inc(norm_step, 1)
                dve.wait_ge(norm_step, 2 * (k * GROUPS + gi) + 1)
                nc.vector.tensor_tensor(y_out[i][:, cols], att_sb[i][:, cols], inv[:], ALU.mult).then_inc(norm_step, 1)
                dve.wait_ge(norm_step, 2 * (k * GROUPS + gi) + 2)
                done = nc.vector.scalar_tensor_tensor(y_out[i][:, cols], y_out[i][:, cols], p.gamma[:], x_res[i][:, cols],
                                                      ALU.mult, ALU.add)
                if is_group(gi, GROUPS - 1):
                    done.then_inc(y_ready, 1)

            with dve.Fori(0, GROUPS // 2) as g2:
                for slot in range(2):
                    tile = 2 * g2 + slot
                    for c in range(2 * GROUP):
                        chunk_max(tile * TILE_USES + c, (slot + c) % 2, slot, c)
                    tile_max(tile * TILE_USES + 2 * GROUP - 1, slot)
                    shift(tile * TILE_USES + 2 * GROUP, slot, tile, 0, tile)

            def run(k, i, pair):
                use = first_use(k)
                last = is_from(k, BLOCKS - 1)
                finishing = not (isinstance(k, int) and k == 0)
                half = pair if i == 1 else pair - 1

                def group(gi, slot, filling):
                    for c in range(2 * GROUP):
                        if c == AHEAD and not last and not is_group(gi, 0):
                            at, bank = shift_use(gi, slot)
                            shift(use + at, bank, (k + 1) * GROUPS + gi - 1, 1 - i, gi - 1)
                        if c == GROUP and finishing:
                            finish(k - 1, 1 - i, half, gi)
                        if not last:
                            at, bank = chunk_use(gi, slot, c)
                            chunk_max(use + at, bank, slot, c)
                    if not last:
                        tile_max(use + at, slot)
                each_group(dve, group)
                if not last:
                    shift(use + LAST_SHIFT, LAST_SHIFT % 2, (k + 2) * GROUPS - 1, 1 - i, GROUPS - 1)
                    use = use + GROUPS * TILE_USES
                for h in range(HALVES):
                    dve.wait_ge(side_full, use + h + 1)
                    nc.vector.tensor_copy(total[:, h * BANK:(h + 1) * BANK], side[h][:]).then_inc(side_free, 1)
                dve.wait_ge(side_free, use + HALVES + 2)
            run(0, 0, 0)
            run(1, 1, 0)
            with dve.Fori(1, BLOCKS // 2 - 1) as pair:
                run(2 * pair, 0, pair)
                run(2 * pair + 1, 1, pair)
            run(BLOCKS - 2, 0, BLOCKS // 2 - 1)
            run(BLOCKS - 1, 1, BLOCKS // 2 - 1)
            for gi in range(GROUPS):
                finish(BLOCKS - 1, 1, BLOCKS // 2 - 1, gi)


def prefix(p):
    nc, B, N, C, H = p.nc, p.B, p.N, p.C, p.HEADS
    D = C
    TILES = 4
    G = TILES * P
    GROUPS = N // G
    ALL = B * GROUPS
    KV = H * D
    ROWS = 2 * H
    W = P + H
    HALF = H // 2
    EARLY = TILES // 2
    EPS = 1e-5
    assert G == BANK and HALF * P == BANK and KV == 2 * BANK and GROUPS % 2 == 0
    with ExitStack() as ctx:
        sb = lambda n, s, dt=F32: ctx.enter_context(nc.sbuf_tensor(n, s, dt))
        ps = lambda n, s: ctx.enter_context(nc.psum_tensor(n, s, F32))
        pair = lambda n, s, dt=F32: [sb(f"{n}{i}", s, dt) for i in range(2)]
        w_high, w_low = sb("w_high", [C, 2 * KV], F32R), sb("w_low", [C, 2 * KV], F32R)
        q_all = sb("q_all", [P, KV])
        tri = sb("tri", [P, P])
        low_r = sb("low_r", [ROWS, 1])
        spread_r = sb("spread_r", [ROWS, H, P], F32R)
        ones_row = sb("ones_row", [ROWS, G])
        minus_half = sb("minus_half", [P, TILES])
        y_in, y_res, t2_sb = pair("y_in", [P, TILES, C]), pair("y_res", [P, TILES, C]), pair("t2_sb", [P, TILES, C])
        stats = sb("stats", [P, TILES, 6])
        both, differ, spread, mean, var = (sb(x, [P, TILES]) for x in ("both", "differ", "spread", "mean", "var"))
        rstd = sb("rstd", [P, TILES])
        tn = sb("tn", [P, TILES, C])
        tn_high, tn_low = sb("tn_high", [C, G], F32R), sb("tn_low", [C, G], F32R)
        k_sb = [sb(f"k_sb{i}", [P, KV]) for i in range(TILES)]
        kq = [sb(f"kq{i}", [P, KV]) for i in range(TILES)]
        v_sb = pair("v_sb", [P, TILES, KV])
        s_tok = sb("s_tok", [P, TILES, H])
        s_rep = sb("s_rep", [P, TILES, 2, H])
        s_row = sb("s_row", [ROWS, G])
        m_row, u_row = pair("m_row", [ROWS, G]), pair("u_row", [ROWS, G])
        less = sb("less", [ROWS, G])
        e_row, inv_u = sb("e_row", [ROWS, G]), sb("inv_u", [ROWS, G])
        r_high, r_parts = sb("r_high", [ROWS, G], F32R), sb("r_parts", [ROWS, G], F32R)
        e_tok = sb("e_tok", [P, TILES, H])
        mat = pair("mat", [P, H, W])
        w_sum = sb("w_sum", [D, H])
        w_turned = sb("w_turned", [H, D])
        o_sb = pair("o_sb", [D, P])
        touched = sb("touched", [1, 2])
        k_ps = [ps(f"k_ps{i}", [P, BANK]) for i in range(2)]
        v_ps = [ps(f"v_ps{i}", [P, BANK]) for i in range(2)]
        a_ps = [ps(f"a_ps{i}", [P, HALF, P]) for i in range(2)]
        even_ps = ps("even_ps", [P, BANK])
        out_ps = ps("out_ps", [P, BANK])
        o_ps = (even_ps, k_ps[0])
        w_turn_ps, tn_ps, s_ps, e_ps = k_ps[1], v_ps[0], v_ps[1], even_ps

        prefix_constants(p, locals())

        names = ("stats_made rstd_made tn_made tn_turned tn_high_made tn_low_made k_made k_taken v_made v_taken "
                 "kq_made s_made s_repeated s_turned s_row_made m_made less_made e_made u_made inv_made r_rounded "
                 "r_parts_made e_turned e_tok_made ve_made ve_late_made a_made mat_made o_made w_added w_turn w_taken o_taken "
                 "o_turned t2_made norm_step").split()
        S = {n: p.sem("px_" + n) for n in names}
        y_in_loaded = [p.sem(f"y_in_loaded{i}") for i in range(2)]
        y_res_loaded = [p.sem(f"y_res_loaded{i}") for i in range(2)]
        t2_stored = [p.sem(f"t2_stored{i}") for i in range(2)]
        CREDITS = {"t2_made": 1}
        block = ctx.enter_context(nc.Block())

        def wait(engine, name, count):
            if not (isinstance(count, int) and count <= 0):
                engine.wait_ge(S[name], count + CREDITS.get(name, 0))

        def each(engine, run):
            def both_of(half, first=False):
                run(2 * half, 0, half, first, False)
                run(2 * half + 1, 1, half, False, first)

            both_of(0, True)
            with engine.Fori(1, B) as b:
                with engine.Fori((b - 1) * (GROUPS // 2) + 1, b * (GROUPS // 2)) as half:
                    both_of(half)
                both_of(b * (GROUPS // 2), True)
            with engine.Fori((B - 1) * (GROUPS // 2) + 1, ALL // 2 - 1) as half:
                both_of(half)
            both_of(ALL // 2 - 1)
            both_of(ALL // 2)

        def stages(n):
            fixed = isinstance(n, int)
            return not fixed or n < ALL, not fixed or 1 <= n <= ALL, not fixed or n >= 2

        def has_next(n):
            return not isinstance(n, int) or n < ALL - 1

        def next_of(i, half):
            return 1 - i, half + i

        @block.sync
        def _(sp):
            def rows_of(dram, first):
                return dram[bass.ds(first, G), :].rearrange("(t p) c -> p t c", p=P)

            def run(n, i, half, first, second):
                new, old, older = stages(n)
                in_at, res_at, out_at = sp.snap((n + 1) * G), sp.snap((n - 1) * G), sp.snap((n - 2) * G)
                if isinstance(n, int) and n == 0:
                    sp.dma_start(y_in[0][:], rows_of(p.y_tok, 0)).then_inc(y_in_loaded[0], DMA)
                if new and has_next(n):
                    wait(sp, "tn_made", n)
                    sp.dma_start(y_in[1 - i][:], rows_of(p.y_tok, in_at)).then_inc(y_in_loaded[1 - i], DMA)
                if old:
                    wait(sp, "t2_made", n - 2)
                    sp.dma_start(y_res[1 - i][:], rows_of(p.y_tok, res_at)).then_inc(y_res_loaded[1 - i], DMA)
                if older:
                    wait(sp, "t2_made", n - 1)
                    sp.dma_start(rows_of(p.t2_d, out_at), t2_sb[i][:]).then_inc(t2_stored[i], DMA)
            each(sp, run)
            for i in range(2):
                sp.wait_ge(t2_stored[i], (ALL // 2 + 1) * DMA)

        @block.tensor
        def _(pe):
            def product(bank, h, tt, first):
                cols = slice(tt * P, (tt + 1) * P)
                passes = ((tn_high, w_high), (tn_low, w_high), (tn_high, w_low))
                for j, (x, w) in enumerate(passes):
                    done = nc.tensor.matmul(bank[h][:], x[:, cols], w[:, first + h * BANK:first + (h + 1) * BANK],
                                            start=j == 0, stop=j == len(passes) - 1)
                return done

            def values(n, tt, between=None):
                wait(pe, "v_taken", n * TILES + tt)
                product(v_ps, 0, tt, KV)
                if tt == 0:
                    between()
                    wait(pe, "s_row_made", n)
                product(v_ps, 1, tt, KV).then_inc(S["v_made"], 1)

            def keys(n, tt):
                wait(pe, "k_taken", n * TILES + tt)
                product(k_ps, 0, tt, 0)
                if tt == 0:
                    wait(pe, "w_taken", (n - 1) * TILES)
                product(k_ps, 1, tt, 0).then_inc(S["k_made"], 1)

            def matrices(t, tt):
                for half in range(2):
                    for j in range(HALF):
                        done = nc.tensor.matmul(a_ps[half][:, j, :], spread_r[:, half * HALF + j, :],
                                                r_parts[:, tt * P:(tt + 1) * P], start=True, stop=True)
                    done.then_inc(S["a_made"], 1)

            def turn_w(t):
                wait(pe, "w_added", t + 1)
                nc.tensor.transpose(w_turn_ps[0:H, 0:D], w_sum[:], p.ident[:]).then_inc(S["w_turn"], 1)

            def turn_o(t, tt):
                wait(pe, "o_taken", t + 1)
                nc.tensor.transpose(out_ps[:, tt * P:(tt + 1) * P], o_sb[tt % 2][:], p.ident[:]).then_inc(S["o_turned"], 1)

            def turn_norm(n):
                wait(pe, "v_taken", n * TILES)
                wait(pe, "tn_made", n + 1)
                for tt in range(TILES):
                    done = nc.tensor.transpose(tn_ps[:, tt * P:(tt + 1) * P], tn[:, tt, :], p.ident[:])
                done.then_inc(S["tn_turned"], 1)

            def turn_s(n):
                wait(pe, "v_taken", (n + 1) * TILES)
                wait(pe, "s_repeated", n + 1)
                for tt in range(TILES):
                    done = nc.tensor.transpose(s_ps[0:ROWS, tt * P:(tt + 1) * P], s_rep[:, tt], p.ident[:])
                done.then_inc(S["s_turned"], 1)

            def weigh(f, i, tt, opens):
                t = f * TILES + tt
                bank = o_ps[tt % 2]
                if tt < EARLY:
                    wait(pe, "ve_made", f * EARLY + tt + 1)
                else:
                    wait(pe, "ve_late_made", f * (TILES - EARLY) + tt - EARLY + 1)
                for h in range(H):
                    done = nc.tensor.matmul(bank[:, 0:W], v_sb[i][:, tt, h * D:(h + 1) * D], mat[tt % 2][:, h, :],
                                            start=h == 0, stop=opens and h == H - 1)
                    if tt > 0 and h == HALF - 1:
                        turn_w(t - 1)
                if tt > 0:
                    turn_o(t - 1, tt - 1)
                if opens:
                    done.then_inc(S["o_made"], 1)
                else:
                    wait(pe, "w_taken", t)
                    nc.tensor.matmul(bank[:, 0:P], w_turned[:], inv_u[0:H, tt * P:(tt + 1) * P],
                                     start=False, stop=True).then_inc(S["o_made"], 1)

            def run(n, i, half, first, second):
                f = n - 1
                new, old, older = stages(n)
                if isinstance(n, int) and n == 0:
                    turn_norm(0)

                def turn_last():
                    if older:
                        turn_w(f * TILES - 1)
                        turn_o(f * TILES - 1, TILES - 1)
                    if old:
                        wait_first(pe, S["tn_made"], (S["e_made"], f + 1))
                        for tt in range(TILES):
                            done = nc.tensor.transpose(e_ps[:, tt * H:(tt + 1) * H], e_row[0:H, tt * P:(tt + 1) * P],
                                                       p.ident[0:H, 0:H])
                        done.then_inc(S["e_turned"], 1)
                if new:
                    wait(pe, "tn_low_made", n + 1)
                    values(n, 0, turn_last)
                else:
                    turn_last()
                if new:
                    for tt in range(TILES - 1):
                        keys(n, tt)
                        values(n, tt + 1)
                        if tt == 1 and old:
                            wait(pe, "r_parts_made", f + 1)
                            matrices(f * TILES, 0)
                elif old:
                    wait(pe, "r_parts_made", f + 1)
                    matrices(f * TILES, 0)
                if new:
                    keys(n, TILES - 1)
                if old:
                    wait(pe, "t2_made", f)
                for tt in range(TILES):
                    if old:
                        t = f * TILES + tt
                        wait(pe, "mat_made", t + 1)
                        if tt < TILES - 1:
                            matrices(t + 1, tt + 1)
                        if tt == 1 and new:
                            wait(pe, "k_taken", (n + 1) * TILES)
                        weigh(f, 1 - i, tt, second and tt == 0)
                    if tt == 0 and new and has_next(n):
                        turn_norm(n + 1)
                    if tt == 1 and new:
                        turn_s(n)
            each(pe, run)

        @block.scalar
        def _(act):
            def touch(function, column):
                nc.scalar.activation(touched[:, column:column + 1], p.ones[0:1, 0:1], function)

            def silu_v(n, i, tt):
                wait(act, "v_made", n * TILES + tt + 1)
                for h in range(2):
                    done = nc.scalar.activation(v_sb[i][:, tt, h * BANK:(h + 1) * BANK], v_ps[h][:], ACT.Silu)
                done.then_inc(S["v_taken"], 1)

            def silu_k(n, i, tt):
                wait(act, "k_made", n * TILES + tt + 1)
                wait(act, "kq_made", (n - 1) * TILES + tt + 1)
                for h in range(2):
                    done = nc.scalar.activation(k_sb[tt][:, h * BANK:(h + 1) * BANK], k_ps[h][:], ACT.Silu)
                done.then_inc(S["k_taken"], 1)

            def take_o(t, tt):
                wait(act, "w_added", t + 1)
                wait(act, "o_turned", t - 1)
                nc.scalar.copy(o_sb[tt % 2][:], o_ps[tt % 2][:, 0:P]).then_inc(S["o_taken"], 1)

            def take_w(t):
                wait(act, "w_turn", t + 1)
                nc.scalar.mul(w_turned[:], w_turn_ps[0:H, 0:D], 1.0 / H).then_inc(S["w_taken"], 1)

            def multiply_e(f, i, tt):
                wait(act, "e_tok_made", f + 1)
                for h in range(H):
                    head = v_sb[i][:, tt, h * D:(h + 1) * D]
                    done = nc.scalar.activation(head, head, ACT.Copy, scale=e_tok[:, tt, h:h + 1])
                done.then_inc(S["ve_late_made"], 1)

            def take_norm(n):
                wait(act, "tn_turned", n + 1)
                nc.scalar.copy(tn_high[:], tn_ps[:]).then_inc(S["tn_high_made"], 1)

            def run(n, i, half, first, second):
                f = n - 1
                new, old, older = stages(n)
                if isinstance(n, int) and n == 0:
                    take_norm(0)
                if older:
                    take_o(f * TILES - 1, TILES - 1)
                if new:
                    touch(ACT.Silu, 0)
                if older:
                    take_w(f * TILES - 1)
                if old:
                    wait(act, "e_turned", f + 1)
                    wait(act, "ve_made", f * EARLY)
                    nc.scalar.copy(e_tok[:].rearrange("p t h -> p (t h)"), e_ps[:, 0:TILES * H]).then_inc(S["e_tok_made"], 1)
                for tt in range(TILES):
                    if new:
                        silu_v(n, i, tt)
                        silu_k(n, i, tt)
                if old:
                    multiply_e(f, 1 - i, 2)
                if old:
                    take_o(f * TILES, 0)
                if new and has_next(n):
                    take_norm(n + 1)
                if old:
                    take_w(f * TILES)
                    multiply_e(f, 1 - i, 3)
                    take_o(f * TILES + 1, 1)
                if new:
                    wait(act, "s_turned", n + 1)
                    nc.scalar.copy(s_row[:], s_ps[0:ROWS, :]).then_inc(S["s_row_made"], 1)
                if old:
                    take_w(f * TILES + 1)
                    take_o(f * TILES + 2, 2)
                    if new:
                        touch(ACT.Exp, 1)
                    take_w(f * TILES + 2)
                if new:
                    wait(act, "less_made", n + 1)
                    wait(act, "u_made", n)
                    nc.scalar.activation(e_row[:], less[:], ACT.Exp).then_inc(S["e_made"], 1)
            each(act, run)

        @block.gpsimd
        def _(pool):
            def inverse_deviation(n):
                wait(pool, "stats_made", n + 1)
                nc.gpsimd.tensor_tensor(rstd[:], var[:], minus_half[:], ALU.pow).then_inc(S["rstd_made"], 1)

            def run(n, i, half, first, second):
                f = n - 1
                new, old, older = stages(n)
                if isinstance(n, int) and n == 0:
                    inverse_deviation(0)

                def multiply_q(tt):
                    if new:
                        wait(pool, "k_taken", n * TILES + tt + 1)
                        wait(pool, "s_made", f * TILES + tt + 1)
                        nc.gpsimd.tensor_tensor(kq[tt][:], k_sb[tt][:], q_all[:], ALU.mult).then_inc(S["kq_made"], 1)

                def multiply_e(tt):
                    if old:
                        v_tile = v_sb[1 - i][:, tt, :].rearrange("p (h d) -> p h d", d=D)
                        nc.gpsimd.tensor_tensor(v_tile, v_tile, e_tok[:, tt, :].unsqueeze(2).to_broadcast([P, H, D]),
                                                ALU.mult).then_inc(S["ve_made"], 1)
                if old:
                    wait(pool, "e_tok_made", f + 1)
                multiply_e(0)
                multiply_q(0)
                multiply_q(1)
                multiply_e(1)
                if new and has_next(n):
                    inverse_deviation(n + 1)
                multiply_q(2)
                multiply_q(3)
            each(pool, run)

        @block.vector
        def _(dve):
            dve.sem_inc(S["t2_made"], CREDITS["t2_made"])
            for i in range(2):
                dve.sem_inc(t2_stored[i], DMA)
            STEPS = 4

            def measure(n, i, half):
                def step(instruction, k):
                    instruction.then_inc(S["norm_step"], 1)
                    dve.wait_ge(S["norm_step"], n * STEPS + k)
                dve.wait_ge(y_in_loaded[i], (half + 1) * DMA)
                for tt in range(TILES):
                    done = nc.vector.bn_stats(stats[:, tt, :], y_in[i][:, tt, :])
                step(done, 1)
                variance(dve, nc, stats, both, differ, spread, mean, var, C, EPS,
                         lambda x, k: step(x, 1 + k)).then_inc(S["stats_made"], 1)

            def normalise(n, i):
                wait(dve, "rstd_made", n + 1)
                for tt in range(TILES):
                    done = nc.vector.tensor_scalar(tn[:, tt, :], y_in[i][:, tt, :], mean[:, tt:tt + 1], rstd[:, tt:tt + 1],
                                                   ALU.subtract, ALU.mult)
                done.then_inc(S["tn_made"], 1)

            def split_norm(n):
                wait(dve, "tn_high_made", n + 1)
                nc.vector.tensor_tensor(tn_low[:], tn_ps[:], plain(tn_high[:]), ALU.subtract).then_inc(S["tn_low_made"], 1)

            def sum_heads(n, tt):
                wait(dve, "kq_made", n * TILES + tt + 1)
                nc.vector.tensor_reduce(s_tok[:, tt, :], kq[tt][:].rearrange("p (h d) -> p h d", d=D), AX.X,
                                        ALU.add).then_inc(S["s_made"], 1)

            def mask(t, tt):
                for half in range(2):
                    wait(dve, "a_made", 2 * t + half + 1)
                    done = nc.vector.tensor_tensor(mat[tt % 2][:, half * HALF:(half + 1) * HALF, 0:P], a_ps[half][:],
                                                   tri[:].unsqueeze(1).to_broadcast([P, HALF, P]), ALU.mult)
                done.then_inc(S["mat_made"], 1)

            def add_w(t, tt, opens=False):
                wait(dve, "o_made", t + 1)
                part = o_ps[tt % 2][:, P:W]
                if opens:
                    nc.vector.tensor_copy(w_sum[:], part).then_inc(S["w_added"], 1)
                else:
                    nc.vector.tensor_tensor(w_sum[:], w_sum[:], part, ALU.add).then_inc(S["w_added"], 1)

            def invert(f, i, opens):
                wait(dve, "e_made", f + 1)
                nc.vector.tensor_tensor_scan(u_row[i][:], ones_row[:], e_row[:], 0.0 if opens else u_row[1 - i][:, G - 1:G],
                                             ALU.mult, ALU.add).then_inc(S["u_made"], 1)
                wait(dve, "u_made", f + 1)
                nc.vector.reciprocal(inv_u[:], u_row[i][:]).then_inc(S["inv_made"], 1)
                wait(dve, "inv_made", f + 1)
                nc.vector.tensor_copy(r_high[:], inv_u[:]).then_inc(S["r_rounded"], 1)
                wait(dve, "r_rounded", f + 1)
                nc.vector.scalar_tensor_tensor(r_parts[:], inv_u[:], low_r[:], plain(r_high[:]), ALU.mult,
                                               ALU.subtract).then_inc(S["r_parts_made"], 1)

            def residual(n, i, half):
                wait(dve, "o_turned", (n + 1) * TILES)
                dve.wait_ge(y_res_loaded[i], (half + 1) * DMA)
                dve.wait_ge(t2_stored[i], (half + 1) * DMA)
                nc.vector.tensor_tensor(t2_sb[i][:].rearrange("p t c -> p (t c)"), out_ps[:],
                                        y_res[i][:].rearrange("p t c -> p (t c)"), ALU.add).then_inc(S["t2_made"], 1)

            def run(n, i, half, first, second):
                f = n - 1
                new, old, older = stages(n)
                if isinstance(n, int) and n == 0:
                    measure(0, 0, 0)
                    normalise(0, 0)
                    split_norm(0)
                if older:
                    add_w(f * TILES - 1, TILES - 1)
                if old:
                    invert(f, 1 - i, second)
                if older:
                    residual(n - 2, i, half - 1)
                if new:
                    sum_heads(n, 0)
                if new and has_next(n):
                    measure(n + 1, *next_of(i, half))
                if new:
                    sum_heads(n, 1)
                if old:
                    mask(f * TILES, 0)
                if new and has_next(n):
                    normalise(n + 1, 1 - i)
                if old:
                    mask(f * TILES + 1, 1)
                if new:
                    sum_heads(n, 2)
                if old:
                    add_w(f * TILES, 0, second)
                    mask(f * TILES + 2, 2)
                if new:
                    sum_heads(n, 3)
                    wait(dve, "s_made", (n + 1) * TILES)
                    nc.vector.tensor_copy(s_rep[:], s_tok[:].unsqueeze(2).to_broadcast([P, TILES, 2, H])).then_inc(S["s_repeated"], 1)
                if new and has_next(n):
                    split_norm(n + 1)
                if old:
                    add_w(f * TILES + 1, 1)
                    mask(f * TILES + 3, 3)
                if new:
                    wait(dve, "s_row_made", n + 1)
                    nc.vector.tensor_tensor_scan(m_row[i][:], s_row[:], s_row[:], -3.0e38 if first else m_row[1 - i][:, G - 1:G],
                                                 ALU.max, ALU.max).then_inc(S["m_made"], 1)
                    wait(dve, "m_made", n + 1)
                    nc.vector.tensor_tensor(less[:], s_row[:], m_row[i][:], ALU.subtract).then_inc(S["less_made"], 1)
                if old:
                    add_w(f * TILES + 2, 2)
            each(dve, run)


def variance(dve, nc, stats, both, differ, spread, mean, var, width, eps, step):
    nc.vector.tensor_tensor(both[:], stats[:, :, 1], stats[:, :, 4], ALU.add)
    nc.vector.tensor_tensor(spread[:], stats[:, :, 2], stats[:, :, 5], ALU.add)
    step(nc.vector.tensor_tensor(differ[:], stats[:, :, 1], stats[:, :, 4], ALU.subtract), 1)
    step(nc.vector.tensor_tensor(differ[:], differ[:], differ[:], ALU.mult), 2)
    nc.vector.tensor_scalar(mean[:], both[:], 0.5, None, ALU.mult)
    step(nc.vector.tensor_scalar(differ[:], differ[:], 0.25, eps, ALU.mult, ALU.add), 3)
    return nc.vector.scalar_tensor_tensor(var[:], spread[:], 1.0 / width, differ[:], ALU.mult, ALU.add)


def prefix_constants(p, v):
    nc, H, C = p.nc, p.HEADS, p.C
    KV = H * C
    WT = 2 * KV // P
    ROWS = 2 * H
    w_in, q_all = v["y_in"], v["q_all"]
    TILES = v["TILES"]
    LOADS = WT // TILES
    loaded = [p.sem(f"wkv_loaded{i}") for i in range(2)]
    q_loaded = p.sem("q_loaded")
    turned, rounded, split = p.sem("wkv_turned"), p.sem("wkv_rounded"), p.sem("wkv_split")
    filled, chosen, stepped = p.sem("pc_filled"), p.sem("pc_chosen"), p.sem("pc_stepped")
    rows = p.ins["L1_attn_W_kv"].rearrange("(n t p) c -> n p t c", p=P, t=TILES)
    banks = v["k_ps"]
    tri, mat = v["tri"], v["mat"]
    bands = v["less"]
    FIRST, SECOND = slice(8, 8 + H), slice(8 + H, 8 + 2 * H)

    def parts(tensor, j):
        return tensor[:].rearrange("c (s h d) -> c s (h d)", s=2, d=C)[:, :, j * (TILES * P // 2):(j + 1) * (TILES * P // 2)]

    with nc.Block() as block:
        @block.sync
        def _(sp):
            sp.dma_start(q_all[:], p.ins["L1_attn_q_proj"].rearrange("h d -> (h d)").partition_broadcast(P)).then_inc(q_loaded, DMA)
            for j in range(LOADS):
                if j >= 2:
                    sp.wait_ge(turned, j - 1)
                sp.dma_start(w_in[j % 2][:], rows[j]).then_inc(loaded[j % 2], DMA)
            sp.wait_ge(q_loaded, DMA)

        @block.tensor
        def _(pe):
            for j in range(LOADS):
                pe.wait_ge(loaded[j % 2], DMA * (j // 2 + 1))
                if j >= 2:
                    pe.wait_ge(split, j - 1)
                for t in range(TILES):
                    done = nc.tensor.transpose(banks[j % 2][:, t * P:(t + 1) * P], w_in[j % 2][:, t, :], p.ident[:])
                done.then_inc(turned, 1)

        @block.vector
        def _(dve):
            for j in range(LOADS):
                source = banks[j % 2][:].rearrange("c (x s) -> c s x", s=2)
                dve.wait_ge(turned, j + 1)
                nc.vector.tensor_copy(parts(v["w_high"], j), source).then_inc(rounded, 1)
                dve.wait_ge(rounded, j + 1)
                nc.vector.tensor_tensor(parts(v["w_low"], j), source, plain(parts(v["w_high"], j)),
                                        ALU.subtract).then_inc(split, 1)
            nc.vector.memset(v["ones_row"][:], 1.0)
            nc.vector.memset(v["minus_half"][:], -0.5)
            dve.wait_ge(chosen, 5)
            nc.vector.tensor_copy(v["low_r"][:], bands[:, 0:1])
            nc.vector.tensor_tensor(bands[:, SECOND], bands[:, SECOND], bands[:, FIRST], ALU.subtract).then_inc(stepped, 1)
            dve.wait_ge(stepped, 1)
            nc.vector.tensor_scalar(v["spread_r"][:], bands[:, SECOND].unsqueeze(2).to_broadcast([ROWS, H, P]), 1.0 / H, None,
                                    ALU.mult)

        @block.gpsimd
        def _(pool):
            nc.gpsimd.memset(tri[:], 1.0).then_inc(filled, 1)
            for i in range(2):
                nc.gpsimd.memset(mat[i][:], 0.0).then_inc(filled, 1)
            nc.gpsimd.memset(bands[:, 0:8], 1.0).then_inc(filled, 1)
            nc.gpsimd.memset(bands[:, 8:8 + ROWS], 0.0).then_inc(filled, 1)
            pool.wait_ge(filled, 5)
            nc.gpsimd.affine_select(out=tri[:], in_=tri[:], compare_op=ALU.is_ge, fill=0.0, base=0,
                                    pattern=[[1, P]], channel_multiplier=-1).then_inc(chosen, 1)
            for i in range(2):
                nc.gpsimd.affine_select(out=mat[i][:, :, P:P + H], in_=mat[i][:, :, P:P + H], compare_op=ALU.not_equal, fill=1.0, base=0,
                                        pattern=[[1, H], [-1, H]], channel_multiplier=0).then_inc(chosen, 1)
            nc.gpsimd.affine_select(out=bands[:, 0:1], in_=bands[:, 0:1], compare_op=ALU.is_ge, fill=0.0, base=-H,
                                    pattern=[[0, 1]], channel_multiplier=1).then_inc(chosen, 1)
            nc.gpsimd.affine_select(out=bands[:, 8:8 + ROWS], in_=bands[:, 8:8 + ROWS],
                                    compare_op=ALU.not_equal, fill=1.0, base=0,
                                    pattern=[[-1, ROWS]], channel_multiplier=1).then_inc(chosen, 1)


def choose(p):
    nc, B, N, C, E = p.nc, p.B, p.N, p.C, p.E
    TILES = 8
    G = TILES * P
    GROUPS = N // G
    BANKS = G // BANK
    K = 8
    TAKEN = -3.0e38
    EPS = 1e-5
    assert TILES * E == BANK and GROUPS % 2 == 0
    p.pooled = p.const("pooled", [C, E, B])
    p.chosen = p.const("chosen", [E, B * N])
    p.scales = p.const("scales", [E, B])
    expert_weights(p)
    with ExitStack() as ctx:
        sb = lambda n, s, dt=F32: ctx.enter_context(nc.sbuf_tensor(n, s, dt))
        ps = lambda n, s: ctx.enter_context(nc.psum_tensor(n, s, F32))
        pair = lambda n, s, dt=F32: [sb(f"{n}{i}", s, dt) for i in range(2)]
        gate_in, gate_w, gate_b = sb("gate_in", [E, C]), sb("gate_w", [C, E]), sb("gate_b", [E, 1])
        t_in = [sb(f"t_in{i}", [P, TILES, C]) for i in range(GROUPS)]
        stats = sb("c_stats", [P, TILES, 6])
        both, differ, spread, minus_half = (sb("c_" + x, [P, TILES]) for x in ("both", "differ", "spread", "minus_half"))
        mean, var, rstd = (pair("c_" + x, [P, TILES]) for x in ("mean", "var", "rstd"))
        tn = sb("c_tn", [P, p.NT, C])
        tn_turned = sb("c_tn_turned", [C, G])
        logits, left, probs = sb("logits", [E, N]), sb("left", [E, N]), sb("c_probs", [E, N])
        top = sb("top", [E, K])
        minus_top, total, scale = sb("minus_top", [E, 1]), sb("total", [E, 1]), sb("scale", [E, 1])
        weights_tok = pair("weights_tok", [P, TILES, E])
        pooled_sb = sb("pooled_sb", [E, C])
        turn_ps = ps("turn_ps", [P, G])
        gate_ps = ps("gate_ps", [P, G])
        w_ps = [ps(f"w_ps{i}", [P, TILES, E]) for i in range(2)]
        pool_ps = ps("pool_ps", [E, C])
        pooled_ps = ps("pooled_ps", [C, E])

        names = ("loaded gate_turned gate_ready filled stats_made rstd_made tn_made turned copied gated logits_made "
                 "maxed topped replaced exped scaled masked kept w_turned w_copied pooled pool_copied "
                 "pool_turned step").split()
        S = {n: p.sem("ch_" + n) for n in names}
        t_loaded = [p.sem(f"t_loaded{i}") for i in range(GROUPS)]
        CREDITS = {"pooled": 2, "w_copied": 2, "pool_turned": 1, "pool_copied": 1}
        block = ctx.enter_context(nc.Block())

        def at(name, count):
            return S[name], count + CREDITS.get(name, 0)

        def wait(engine, name, count):
            sem, value = at(name, count)
            if not (isinstance(value, int) and value <= 0):
                engine.wait_ge(sem, value)

        def credit(engine, *which):
            for name in which:
                engine.sem_inc(S[name], CREDITS[name])

        def images(engine, run):
            run(0, True, False)
            with engine.Fori(1, B - 1) as b:
                run(b, True, True)
            run(B - 1, True, True)
            run(B, False, True)

        @block.sync
        def _(sp):
            sp.dma_start(gate_in[:], p.ins["L1_ffn_gate_w"]).then_inc(S["loaded"], DMA)
            sp.dma_start(gate_b[:], p.ins["L1_ffn_gate_b"].rearrange("(e o) -> e o", o=1)).then_inc(S["loaded"], DMA)

            def load(n, i):
                sp.dma_start(t_in[i][:], p.t2_d[bass.ds(n * G, G), :].rearrange("(t p) c -> p t c", p=P)).then_inc(t_loaded[i], DMA)
            for g in range(GROUPS):
                load(g, g)
            for i in range(2):
                load_w1(p, sp, i * p.EG, i)
                load_w2(p, sp, i * p.EG, i)
            with sp.Fori(1, B) as b:
                for g in range(GROUPS):
                    n = b * GROUPS + g
                    at = sp.snap(n * G)
                    wait(sp, "tn_made", n - GROUPS + 1)
                    sp.dma_start(t_in[g][:], p.t2_d[bass.ds(at, G), :].rearrange("(t p) c -> p t c", p=P)).then_inc(t_loaded[g], DMA)

        @block.tensor
        def _(pe):
            pe.wait_ge(S["loaded"], 2 * DMA)
            nc.tensor.transpose(pooled_ps[:], gate_in[:], p.ident[0:E, 0:E]).then_inc(S["gate_turned"], 1)
            pe.wait_ge(S["gate_ready"], 1)
            credit(pe, "pooled", "pool_turned")

            def turn_weights(m, g):
                wait_first(pe, S["gate_ready"], at("masked", m + 1), at("w_copied", m - 1))
                for tt in range(TILES):
                    first = g * G + tt * P
                    done = nc.tensor.transpose(w_ps[g % 2][:, tt, :], probs[:, first:first + P], p.ident[0:E, 0:E])
                done.then_inc(S["w_turned"], 1)

            def pool_tokens(m, g):
                wait_first(pe, S["gate_ready"], at("w_copied", m + 1))
                for tt in range(TILES):
                    done = nc.tensor.matmul(pool_ps[:], weights_tok[g % 2][:, tt, :], tn[:, g * TILES + tt, :],
                                            start=g == 0 and tt == 0, stop=g == GROUPS - 1 and tt == TILES - 1,
                                            skip_group_check=True)
                done.then_inc(S["pooled"], 1)

            def run(b, gating, pooling):
                before = (b - 1) * GROUPS
                if pooling:
                    turn_weights(before, 0)
                    turn_weights(before + 1, 1)
                    wait(pe, "pool_copied", b - 1)
                    pool_tokens(before, 0)
                for g in range(GROUPS):
                    n = b * GROUPS + g
                    if gating:
                        wait(pe, "copied", n)
                        wait(pe, "tn_made", n + 1)
                        for tt in range(TILES):
                            done = nc.tensor.transpose(turn_ps[:, tt * P:(tt + 1) * P], tn[:, g * TILES + tt, :], p.ident[:])
                        done.then_inc(S["turned"], 1)
                    if pooling and g + 1 < GROUPS:
                        pool_tokens(before + g + 1, g + 1)
                    if pooling and g + 2 < GROUPS:
                        turn_weights(before + g + 2, g + 2)
                    if gating:
                        wait(pe, "copied", n + 1)
                        wait(pe, "logits_made", n)
                        for h in range(BANKS):
                            cols = slice(h * BANK, (h + 1) * BANK)
                            done = nc.tensor.matmul(gate_ps[0:E, cols], gate_w[:], tn_turned[:, cols], start=True, stop=True)
                        done.then_inc(S["gated"], 1)
                if pooling:
                    wait_first(pe, S["gate_ready"], at("pool_copied", b))
                    nc.tensor.transpose(pooled_ps[:], pooled_sb[:], p.ident[0:E, 0:E]).then_inc(S["pool_turned"], 1)
            images(pe, run)

        @block.scalar
        def _(act):
            credit(act, "w_copied", "pool_copied")
            act.wait_ge(S["gate_turned"], 1)
            nc.scalar.copy(gate_w[:], pooled_ps[:]).then_inc(S["gate_ready"], 1)

            def take_weights(m, g):
                wait(act, "w_turned", m + 1)
                wait(act, "pooled", m - 1)
                nc.scalar.copy(weights_tok[g % 2][:], w_ps[g % 2][:]).then_inc(S["w_copied"], 1)

            def run(b, gating, pooling):
                before = (b - 1) * GROUPS
                if pooling:
                    take_weights(before, 0)
                    take_weights(before + 1, 1)
                for g in range(GROUPS):
                    n = b * GROUPS + g
                    if gating:
                        wait(act, "turned", n + 1)
                        wait(act, "gated", n)
                        for h in range(BANKS):
                            cols = slice(h * BANK, (h + 1) * BANK)
                            done = nc.scalar.copy(tn_turned[:, cols], turn_ps[:, cols])
                        done.then_inc(S["copied"], 1)
                    if pooling and g + 2 < GROUPS:
                        take_weights(before + g + 2, g + 2)
                    if gating:
                        wait(act, "gated", n + 1)
                        if g == 0:
                            wait(act, "replaced", b)
                        for h in range(BANKS):
                            cols = slice(h * BANK, (h + 1) * BANK)
                            done = nc.scalar.activation(logits[:, g * G + h * BANK:g * G + (h + 1) * BANK], gate_ps[0:E, cols],
                                                        ACT.Identity, bias=gate_b[:])
                        done.then_inc(S["logits_made"], 1)
                if pooling:
                    wait(act, "pooled", b * GROUPS)
                    wait(act, "pool_turned", b - 1)
                    nc.scalar.activation(pooled_sb[:], pool_ps[:], ACT.Copy, scale=scale[:]).then_inc(S["pool_copied"], 1)
                if gating:
                    wait(act, "kept", b * GROUPS)
                    wait(act, "topped", b + 1)
                    nc.scalar.activation(probs[:], logits[:], ACT.Exp, bias=minus_top[:], accum_out=total[:]).then_inc(S["exped"], 1)
            images(act, run)

        @block.gpsimd
        def _(pool):
            pool.wait_ge(S["filled"], 1)

            def run(b, gating, pooling):
                for g in range(GROUPS):
                    if gating:
                        wait(pool, "stats_made", b * GROUPS + g + 1)
                        nc.gpsimd.tensor_tensor(rstd[g % 2][:], var[g % 2][:], minus_half[:], ALU.pow).then_inc(S["rstd_made"], 1)
                    if pooling:
                        wait_first(pool, S["filled"], at("masked", (b - 1) * GROUPS + g + 1))
                        nc.gpsimd.tensor_copy(p.chosen[:, bass.ds((b - 1) * N + g * G, G)],
                                              probs[:, g * G:(g + 1) * G]).then_inc(S["kept"], 1)
            images(pool, run)

        @block.vector
        def _(dve):
            nc.vector.memset(minus_half[:], -0.5).then_inc(S["filled"], 1)
            STEPS = 4

            def measure(b, g):
                n = b * GROUPS + g

                def step(x, k):
                    x.then_inc(S["step"], 1)
                    dve.wait_ge(S["step"], n * STEPS + k)
                dve.wait_ge(t_loaded[g], (b + 1) * DMA)
                for tt in range(TILES):
                    done = nc.vector.bn_stats(stats[:, tt, :], t_in[g][:, tt, :])
                step(done, 1)
                variance(dve, nc, stats, both, differ, spread, mean[g % 2], var[g % 2], C, EPS,
                         lambda x, k: step(x, 1 + k)).then_inc(S["stats_made"], 1)

            def run(b, gating, pooling):
                if gating:
                    if isinstance(b, int) and b == 0:
                        measure(0, 0)
                    for g in range(GROUPS):
                        n = b * GROUPS + g
                        if g + 1 < GROUPS:
                            measure(b, g + 1)
                        wait(dve, "rstd_made", n + 1)
                        if pooling:
                            wait(dve, "pooled", (b - 1) * GROUPS + g + 1)
                        for tt in range(TILES):
                            done = nc.vector.tensor_scalar(tn[:, g * TILES + tt, :], t_in[g][:, tt, :], mean[g % 2][:, tt:tt + 1],
                                                           rstd[g % 2][:, tt:tt + 1], ALU.subtract, ALU.mult)
                        done.then_inc(S["tn_made"], 1)
                    if not (isinstance(b, int) and b == B - 1):
                        measure(b + 1, 0)
                if pooling:
                    wait(dve, "pool_turned", b)
                    nc.vector.tensor_copy(p.pooled[:, :, bass.ds(b - 1, 1)].rearrange("c e o -> c (e o)"), pooled_ps[:])
                if gating:
                    wait_first(dve, S["filled"], at("logits_made", (b + 1) * GROUPS))
                    nc.vector.max(top[:], logits[:]).then_inc(S["maxed"], 1)
                    wait(dve, "maxed", b + 1)
                    nc.vector.tensor_scalar(minus_top[:], top[:, 0:1], -1.0, None, ALU.mult).then_inc(S["topped"], 1)
                    nc.vector.match_replace(left[:], top[:], logits[:], TAKEN).then_inc(S["replaced"], 1)
                    wait(dve, "exped", b + 1)
                    nc.vector.reciprocal(scale[:], total[:]).then_inc(S["scaled"], 1)
                    wait(dve, "scaled", b + 1)
                    nc.vector.tensor_copy(p.scales[:, bass.ds(b, 1)], scale[:])
                    wait(dve, "replaced", b + 1)
                    for g in range(GROUPS):
                        cols = slice(g * G, (g + 1) * G)
                        nc.vector.scalar_tensor_tensor(probs[:, cols], left[:, cols], TAKEN, probs[:, cols], ALU.is_le,
                                                       ALU.mult).then_inc(S["masked"], 1)
            images(dve, run)


def expert_weights(p):
    C, HID = p.C, p.ins["L1_ffn_weight1"].shape[2]
    KC = HID // P
    p.w1_sb = [p.const(f"w1_sb{i}", [C, p.EG, HID]) for i in range(2)]
    p.w2_sb = [p.const(f"w2_sb{i}", [P, p.EG, KC, C]) for i in range(2)]
    p.w_loaded = [p.sem(f"w_loaded{i}") for i in range(4)]


def load_w1(p, sp, first, i):
    rows = p.ins["L1_ffn_weight1"][bass.ds(first, p.EG), 0:p.C, :]
    sp.dma_start(p.w1_sb[i][:], rows.rearrange("e c h -> c e h")).then_inc(p.w_loaded[i], DMA)


def load_w2(p, sp, first, i):
    hidden = p.ins["L1_ffn_weight1"].shape[2]
    rows = p.ins["L1_ffn_weight2"][bass.ds(first, p.EG), 0:hidden, :]
    sp.dma_start(p.w2_sb[i][:], rows.rearrange("e (p k) c -> p e k c", p=P)).then_inc(p.w_loaded[i], DMA)


def experts(p):
    nc, B, C, E, EG = p.nc, p.B, p.C, p.E, p.EG
    HID = p.ins["L1_ffn_weight1"].shape[2]
    SIDE = P // EG
    GROUPS = E // EG
    KC = HID // P
    SLOTS = len(p.w_loaded)
    assert HID == BANK and KC * C == BANK and GROUPS % SLOTS == 0
    w1 = p.ins["L1_ffn_weight1"]
    with ExitStack() as ctx:
        sb = lambda n, s, dt=F32: ctx.enter_context(nc.sbuf_tensor(n, s, dt))
        ps = lambda n, s: ctx.enter_context(nc.psum_tensor(n, s, F32))
        for i in range(len(p.w1_sb), SLOTS):
            p.w1_sb.append(sb(f"w1_sb{i}", [C, EG, HID]))
            p.w2_sb.append(sb(f"w2_sb{i}", [P, EG, KC, C]))
        w1_sb, w2_sb, w_loaded = p.w1_sb, p.w2_sb, p.w_loaded
        b1_sb = [sb(f"b1_sb{i}", [P, HID]) for i in range(2)]
        pooled_g = [sb(f"pooled_g{i}", [C, EG, SIDE]) for i in range(2)]
        pre = [sb(f"pre{i}", [P, HID]) for i in range(2)]
        hid = [sb(f"hid{i}", [P, HID]) for i in range(2)]
        hid_turned = [sb(f"hid_turned{i}", [P, KC, P]) for i in range(2)]
        out_all = sb("out_all", [P, GROUPS, C])
        h_ps = [ps(f"h_ps{i}", [P, HID]) for i in range(2)]
        t_ps = [ps(f"t_ps{i}", [P, KC, P]) for i in range(2)]
        o_ps = [ps(f"e_o_ps{i}", [P, C]) for i in range(2)]
        b1_loaded = [p.sem(f"b1_loaded{i}") for i in range(2)]
        names = ("cleared gathered first added geluted turned taken second kept stored").split()
        S = {n: p.sem("ex_" + n) for n in names}
        CREDITS = {"first": 2, "second": 2, "added": 2, "taken": 2, "kept": 2, "geluted": 2, "turned": 2}
        block = ctx.enter_context(nc.Block())

        def at(name, count):
            return S[name], count + CREDITS.get(name, 0)

        def wait(engine, name, count):
            engine.wait_ge(*at(name, count))

        def credit(engine, *which):
            for name in which:
                engine.sem_inc(S[name], CREDITS[name])

        def groups(engine, run):
            with engine.Fori(0, GROUPS // SLOTS - 1) as filling:
                for slot in range(SLOTS):
                    run(SLOTS * filling + slot, slot, filling)
            for slot in range(SLOTS):
                run(GROUPS - SLOTS + slot, slot, GROUPS // SLOTS - 1)

        def has_next(g):
            return not isinstance(g, int) or g < GROUPS - 1

        def next_of(slot, filling):
            return (slot + 1) % SLOTS, filling + (slot + 1) // SLOTS

        @block.sync
        def _(sp):
            for i in range(2, SLOTS):
                load_w1(p, sp, i * EG, i)
                load_w2(p, sp, i * EG, i)
            with sp.Fori(1, GROUPS // SLOTS) as filling:
                for slot in range(SLOTS):
                    g = SLOTS * filling + slot
                    first = sp.snap(g * EG)
                    wait(sp, "first", g - SLOTS + 1)
                    load_w1(p, sp, first, slot)
                    first = sp.snap(g * EG)
                    wait(sp, "second", g - SLOTS + 1)
                    load_w2(p, sp, first, slot)

        @block.tensor
        def _(pe):
            credit(pe, "first", "second", "turned")

            def first_layer(g, i, slot, filling):
                wait_first(pe, S["cleared"], at("gathered", g + 1), at("added", g - 1), (w_loaded[slot], (filling + 1) * 2 * DMA))
                for j in range(EG):
                    done = nc.tensor.matmul(h_ps[i][j * SIDE:(j + 1) * SIDE, :], pooled_g[i][:, j, :], w1_sb[slot][:, j, :],
                                            start=True, stop=True)
                done.then_inc(S["first"], 1)

            def run(g, slot, filling):
                i = slot % 2
                if has_next(g):
                    first_layer(g + 1, 1 - i, *next_of(slot, filling))
                wait(pe, "geluted", g + 1)
                wait(pe, "taken", g - 1)
                for k in range(KC):
                    done = nc.tensor.transpose(t_ps[i][:, k, :], hid[i][:].rearrange("p (q k) -> p k q", k=KC)[:, k, :], p.ident[:])
                done.then_inc(S["turned"], 1)
                wait_first(pe, S["cleared"], at("taken", g + 1), at("kept", g - 1))
                for j in range(EG):
                    for k in range(KC):
                        done = nc.tensor.matmul(o_ps[i][j * SIDE:(j + 1) * SIDE, :], hid_turned[i][:, k, j * SIDE:(j + 1) * SIDE],
                                                w2_sb[slot][:, j, k, :], start=k == 0, stop=k == KC - 1)
                done.then_inc(S["second"], 1)
            first_layer(0, 0, 0, 0)
            groups(pe, run)

        @block.vector
        def _(dve):
            credit(dve, "added", "kept")
            for i in range(2):
                nc.vector.memset(pooled_g[i][:], 0.0)
                done = nc.vector.memset(b1_sb[i][:], 0.0)
            done.then_inc(S["cleared"], 1)
            dve.wait_ge(S["cleared"], 1)

            def gather(g, i):
                wait(dve, "first", g - 1)
                nc.vector.tensor_copy(pooled_g[i][:, :, 0:B], p.pooled[:, bass.ds(g * EG, EG), :]).then_inc(S["gathered"], 1)

            def run(g, slot, filling):
                i = slot % 2
                if has_next(g):
                    gather(g + 1, 1 - i)
                wait(dve, "first", g + 1)
                wait(dve, "geluted", g - 1)
                dve.wait_ge(b1_loaded[i], (filling * (SLOTS // 2) + slot // 2 + 1) * EG * DMA)
                nc.vector.tensor_tensor(pre[i][:], h_ps[i][:], b1_sb[i][:], ALU.add).then_inc(S["added"], 1)
                wait(dve, "second", g + 1)
                nc.vector.tensor_copy(out_all[:, bass.ds(g, 1), :].rearrange("p o c -> p (o c)"), o_ps[i][:]).then_inc(S["kept"], 1)
            gather(0, 0)
            groups(dve, run)

        @block.scalar
        def _(act):
            credit(act, "taken", "geluted")
            act.wait_ge(S["cleared"], 1)

            def load_bias(g, i):
                for j in range(EG):
                    wait(act, "added", g - 1)
                    act.dma_start(b1_sb[i][j * SIDE:j * SIDE + B, :],
                                  w1[bass.ds(g * EG + j, 1), C, :].rearrange("o h -> (o h)").partition_broadcast(B)).then_inc(b1_loaded[i], DMA)

            def run(g, slot, filling):
                i = slot % 2
                if has_next(g):
                    load_bias(g + 1, 1 - i)
                wait(act, "added", g + 1)
                wait(act, "turned", g - 1)
                nc.scalar.activation(hid[i][:], pre[i][:], ACT.Gelu).then_inc(S["geluted"], 1)
                wait(act, "turned", g + 1)
                wait(act, "second", g - 1)
                nc.scalar.copy(hid_turned[i][:], t_ps[i][:]).then_inc(S["taken"], 1)
            load_bias(0, 0)
            groups(act, run)
            wait(act, "kept", GROUPS)
            for j in range(EG):
                act.dma_start(p.expert_d.rearrange("(g j) b c -> j b g c", j=EG)[j],
                              out_all[j * SIDE:j * SIDE + B, :, :]).then_inc(S["stored"], DMA)
            act.wait_ge(S["stored"], EG * DMA)


def combine(p):
    nc, B, N, C, E = p.nc, p.B, p.N, p.C, p.E
    HID = p.ins["L1_ffn_weight1"].shape[2]
    TILES = 4
    G = TILES * P
    GROUPS = N // G
    SLOTS = 4
    out_v = p.out.rearrange("b h w c -> (b h w) c")
    assert GROUPS % SLOTS == 0
    with ExitStack() as ctx:
        sb = lambda n, s, dt=F32: ctx.enter_context(nc.sbuf_tensor(n, s, dt))
        outs, b2 = sb("outs", [E, B, C]), sb("b2", [E, C])
        weights = [sb(f"f_weights{i}", [E, G]) for i in range(2)]
        tokens = [sb(f"f_tokens{i}", [P, TILES, C]) for i in range(SLOTS)]
        result = [sb(f"result{i}", [P, TILES, C]) for i in range(SLOTS)]
        acc = [ctx.enter_context(nc.psum_tensor(f"acc{i}", [P, TILES, C], F32)) for i in range(2)]
        ready, made, added, copied = p.sem("fi_ready"), p.sem("fi_made"), p.sem("fi_added"), p.sem("fi_copied")
        outs_loaded, outs_step = p.sem("outs_loaded"), p.sem("outs_step")
        loaded = [p.sem(f"fi_loaded{i}") for i in range(SLOTS)]
        stored = [p.sem(f"fi_stored{i}") for i in range(SLOTS)]
        block = ctx.enter_context(nc.Block())

        @block.sync
        def _(sp):
            sp.dma_start(outs[:], p.expert_d).then_inc(outs_loaded, DMA)
            sp.dma_start(b2[:], p.ins["L1_ffn_weight2"][:, HID, :]).then_inc(outs_loaded, DMA)
            with sp.Fori(0, B * GROUPS // SLOTS) as n4:
                for i in range(SLOTS):
                    n = SLOTS * n4 + i
                    at = sp.snap(n * G)
                    sp.wait_ge(added, n + 1)
                    sp.dma_start(tokens[i][:], p.t2_d[bass.ds(at, G), :].rearrange("(t p) c -> p t c", p=P)).then_inc(loaded[i], DMA)

        @block.gpsimd
        def _(pool):
            with pool.Fori(0, B * GROUPS // 2) as n2:
                for i in range(2):
                    n = 2 * n2 + i
                    wait_first(pool, ready, (made, n + 1))
                    nc.gpsimd.tensor_copy(weights[i][:], p.chosen[:, bass.ds(n * G, G)]).then_inc(copied, 1)

        @block.tensor
        def _(pe):
            pe.sem_inc(made, 2)
            pe.wait_ge(ready, 1)
            with pe.Fori(0, B) as b:
                with pe.Fori(0, GROUPS // 2) as g2:
                    for i in range(2):
                        n = b * GROUPS + 2 * g2 + i
                        wait_first(pe, ready, (added, n - 1 + SLOTS), (copied, n + 1))
                        for tt in range(TILES):
                            done = nc.tensor.matmul(acc[i][:, tt, :], weights[i][:, tt * P:(tt + 1) * P], outs[:, bass.ds(b, 1), :],
                                                    start=True, stop=True)
                        done.then_inc(made, 1)

        @block.vector
        def _(dve):
            dve.sem_inc(added, SLOTS)
            for i in range(SLOTS):
                dve.sem_inc(stored[i], DMA)
            dve.wait_ge(outs_loaded, 2 * DMA)
            nc.vector.tensor_tensor(outs[:], outs[:], b2[:].unsqueeze(1).to_broadcast([E, B, C]), ALU.add).then_inc(outs_step, 1)
            dve.wait_ge(outs_step, 1)
            nc.vector.tensor_tensor(outs[:], outs[:], p.scales[:].unsqueeze(2).to_broadcast([E, B, C]), ALU.mult).then_inc(ready, 1)
            with dve.Fori(0, B * GROUPS // SLOTS) as n4:
                for i in range(SLOTS):
                    n = SLOTS * n4 + i
                    dve.wait_ge(made, n + 1 + 2)
                    dve.wait_ge(loaded[i], (n4 + 1) * DMA)
                    dve.wait_ge(stored[i], (n4 + 1) * DMA)
                    nc.vector.tensor_tensor(result[i][:], acc[i % 2][:], tokens[i][:], ALU.add).then_inc(added, 1)

        @block.scalar
        def _(act):
            with act.Fori(0, B * GROUPS // SLOTS) as n4:
                for i in range(SLOTS):
                    n = SLOTS * n4 + i
                    act.wait_ge(added, n + 1 + SLOTS)
                    act.dma_start(out_v[bass.ds(n * G, G), :].rearrange("(t p) c -> p t c", p=P), result[i][:]).then_inc(stored[i], DMA)
            for i in range(SLOTS):
                act.wait_ge(stored[i], (B * GROUPS // SLOTS + 1) * DMA)


INPUTS = ["x", "L0_conv_Wq", "L0_conv_Wk", "L0_conv_Wv", "L0_conv_gamma", "L1_attn_W_kv", "L1_attn_q_proj",
          "L1_ffn_gate_w", "L1_ffn_gate_b", "L1_ffn_weight1", "L1_ffn_weight2"]


def program(nc, ins, out):
    with ExitStack() as whole:
        p = Program(nc, whole, ins, out)
        prepare(p)
        project(p)
        pairs(p)
        prefix(p)
        choose(p)
        experts(p)
        combine(p)


def kernel(**inputs):
    import numpy as np
    import concourse.bacc as bacc
    from concourse.bass_utils import run_bass_kernel_spmd

    nc = bacc.Bacc("TRN2", target_bir_lowering=False, num_devices=1)
    arrays, ins = {}, {}
    for name in INPUTS:
        a = np.ascontiguousarray(inputs[name])
        a = a.reshape(a.shape or (1,))
        arrays[f"in_{name}"] = a
        ins[name] = nc.dram_tensor(f"in_{name}", a.shape, mybir.dt.from_np(a.dtype), kind="ExternalInput").ap()
    out = nc.dram_tensor("out_0", inputs["x"].shape, F32, kind="ExternalOutput").ap()
    program(nc, ins, out)
    r = run_bass_kernel_spmd(nc, [arrays], core_ids=[0])
    return r.results[0]["out_0"]
```
